# Optimizing a Trainium2 kernel written in Bass

```python
import numpy as np
import jax
import jax.numpy as jnp

def _softmax(x, axis=-1):
    return jax.nn.softmax(x, axis=axis)

def _gelu(x):
    return jax.nn.gelu(x, approximate=True)

def _silu(x):
    return jax.nn.silu(x)

def _sigmoid(x):
    return jax.nn.sigmoid(x)

def _layernorm(x, axis=-1, eps=1e-05):
    m = jnp.mean(x, axis=axis, keepdims=True)
    v = jnp.var(x, axis=axis, keepdims=True)
    return (x - m) / jnp.sqrt(v + eps)

def _scatter_add(tgt, idx, src, axis=0):
    return tgt.at[idx].add(src)

def _segment_sum(src, seg, n):
    return jax.ops.segment_sum(src, seg, n)
kernel_name = 'mk_adaln_d1_jaxref_r8_700f6c'

def setup_inputs(seed: int=0):
    np.random.seed(seed)
    _w = jnp.asarray

    def _L0_attn_setup():
        import jax, jax.numpy as jnp
        import numpy as np
        HID = 128
        NH = 16
        HD = HID // NH
        RD = int(HD * 0.25)
        B = 2
        S = 256
        ROPE_BASE = 10000.0

        def _rotary_tables(seq_len):
            inv_freq = 1.0 / ROPE_BASE ** (jnp.arange(0, RD, 2, dtype=jnp.float32) / RD)
            t = jnp.arange(seq_len, dtype=jnp.float32)
            freqs = jnp.outer(t, inv_freq)
            emb = jnp.concatenate([freqs, freqs], axis=-1)
            return (jnp.cos(emb)[None, None], jnp.sin(emb)[None, None])

        def _rotate_half(x):
            x1, x2 = jnp.split(x, 2, axis=-1)
            return jnp.concatenate([-x2, x1], axis=-1)
        key = jax.random.key(seed)
        ks = jax.random.split(key, 4)
        hidden_states = jax.random.normal(ks[0], (B, S, HID), jnp.float32)
        Wqkv = jax.random.normal(ks[1], (3 * HID, HID), jnp.float32) * HID ** (-0.5)
        bqkv = jnp.zeros((3 * HID,), jnp.float32)
        Wd = jax.random.normal(ks[2], (HID, HID), jnp.float32) * HID ** (-0.5)
        bd = jnp.zeros((HID,), jnp.float32)
        return {'hidden_states': hidden_states, 'Wqkv': Wqkv, 'bqkv': bqkv, 'Wd': Wd, 'bd': bd}
    _L0_attn_in = _L0_attn_setup()

    def _L0_ffn_setup():
        import jax, jax.numpy as jnp
        import numpy as np
        HID = 128
        INTER = 512
        RDIM = 128
        HEADS = 4
        NUM_EXPERTS = 2048
        NUM_KEYS = 128
        TOPK = 8
        B, T = (2, 256)
        key = jax.random.key(seed)
        ks = jax.random.split(key, 8)
        s = lambda fan_in: 1.0 / np.sqrt(fan_in)
        return {'hidden_states': jax.random.normal(ks[0], (B, T, HID), jnp.float32), 'Wq': jax.random.normal(ks[1], (HEADS * RDIM, HID), jnp.float32) * s(HID), 'keys': jax.random.normal(ks[2], (HEADS, NUM_KEYS, 2, RDIM // 2), jnp.float32) * s(RDIM // 2), 'down_embed': jax.random.normal(ks[3], (NUM_EXPERTS, HID), jnp.float32) * 0.02, 'up_embed': jax.random.normal(ks[4], (NUM_EXPERTS, HID), jnp.float32) * 0.02, 'Wg': jax.random.normal(ks[5], (INTER, HID), jnp.float32) * s(HID), 'Wu': jax.random.normal(ks[6], (INTER, HID), jnp.float32) * s(HID), 'Wd': jax.random.normal(ks[7], (HID, INTER), jnp.float32) * s(INTER)}
    _L0_ffn_in = _L0_ffn_setup()
    _L0_c = _w((lambda *s: np.random.randn(*s).astype(np.float32) * 0.05)(4, 128))
    _L0_wmod = _w((lambda *s: np.random.randn(*s).astype(np.float32) * 0.05)(128, 6 * 128) * 128 ** (-0.5))
    _d = {'L0_attn_hidden_states': _L0_attn_in['hidden_states'], 'L0_attn_Wqkv': _L0_attn_in['Wqkv'], 'L0_attn_bqkv': _L0_attn_in['bqkv'], 'L0_attn_Wd': _L0_attn_in['Wd'], 'L0_attn_bd': _L0_attn_in['bd'], 'L0_ffn_Wq': _L0_ffn_in['Wq'], 'L0_ffn_keys': _L0_ffn_in['keys'], 'L0_ffn_down_embed': _L0_ffn_in['down_embed'], 'L0_ffn_up_embed': _L0_ffn_in['up_embed'], 'L0_ffn_Wg': _L0_ffn_in['Wg'], 'L0_ffn_Wu': _L0_ffn_in['Wu'], 'L0_ffn_Wd': _L0_ffn_in['Wd'], 'L0_c': _L0_c, 'L0_wmod': _L0_wmod}
    _x0 = _d['L0_attn_hidden_states']
    _d['L0_attn_hidden_states'] = jax.random.normal(jax.random.fold_in(jax.random.key(seed), 1), (4, 1024, 128), dtype=_x0.dtype)
    del _x0
    return _d

def reference(L0_attn_hidden_states, L0_attn_Wqkv, L0_attn_bqkv, L0_attn_Wd, L0_attn_bd, L0_ffn_Wq, L0_ffn_keys, L0_ffn_down_embed, L0_ffn_up_embed, L0_ffn_Wg, L0_ffn_Wu, L0_ffn_Wd, L0_c, L0_wmod):

    def _L0_attn_ref(hidden_states, Wqkv, bqkv, Wd, bd):
        import jax, jax.numpy as jnp
        import numpy as np
        HID = 128
        NH = 16
        HD = HID // NH
        RD = int(HD * 0.25)
        B = 2
        S = 256
        ROPE_BASE = 10000.0

        def _rotary_tables(seq_len):
            inv_freq = 1.0 / ROPE_BASE ** (jnp.arange(0, RD, 2, dtype=jnp.float32) / RD)
            t = jnp.arange(seq_len, dtype=jnp.float32)
            freqs = jnp.outer(t, inv_freq)
            emb = jnp.concatenate([freqs, freqs], axis=-1)
            return (jnp.cos(emb)[None, None], jnp.sin(emb)[None, None])

        def _rotate_half(x):
            x1, x2 = jnp.split(x, 2, axis=-1)
            return jnp.concatenate([-x2, x1], axis=-1)
        b, s, _ = hidden_states.shape
        qkv = hidden_states @ Wqkv.T + bqkv
        qkv = qkv.reshape(b, s, 3, NH, HD).transpose(2, 0, 3, 1, 4)
        q, k, v = (qkv[0], qkv[1], qkv[2])
        cos, sin = _rotary_tables(s)
        q_rot, q_pass = (q[..., :RD], q[..., RD:])
        k_rot, k_pass = (k[..., :RD], k[..., RD:])
        q_rot = q_rot * cos + _rotate_half(q_rot) * sin
        k_rot = k_rot * cos + _rotate_half(k_rot) * sin
        q = jnp.concatenate([q_rot, q_pass], axis=-1)
        k = jnp.concatenate([k_rot, k_pass], axis=-1)
        scale = HD ** (-0.5)
        logits = jnp.einsum('bhqd,bhkd->bhqk', q, k) * scale
        causal_mask = jnp.triu(jnp.full((s, s), -jnp.inf, dtype=logits.dtype), 1)
        probs = jax.nn.softmax(logits + causal_mask, axis=-1)
        L = jnp.eye(s, dtype=probs.dtype) - jnp.tril(probs, -1)
        rhs = jnp.diagonal(probs, axis1=-2, axis2=-1)[..., None] * v
        A = jax.scipy.linalg.solve_triangular(L, rhs, lower=True)
        attn_output = A.transpose(0, 2, 1, 3).reshape(b, s, HID)
        return attn_output @ Wd.T + bd

    def _L0_ffn_ref(hidden_states, Wq, keys, down_embed, up_embed, Wg, Wu, Wd):
        import jax, jax.numpy as jnp
        import numpy as np
        HID = 128
        INTER = 512
        RDIM = 128
        HEADS = 4
        NUM_EXPERTS = 2048
        NUM_KEYS = 128
        TOPK = 8
        B, T = (2, 256)
        b, t, _ = hidden_states.shape
        q = hidden_states @ Wq.T
        q = q.reshape(b, t, 2, HEADS, RDIM // 2)
        q = jnp.transpose(q, (2, 0, 1, 3, 4))
        sim = jnp.einsum('pbthn,hkpn->pbthk', q, keys)
        sx, ix = jax.lax.top_k(sim[0], TOPK)
        sy, iy = jax.lax.top_k(sim[1], TOPK)
        all_scores = (sx[..., :, None] + sy[..., None, :]).reshape(b, t, HEADS, TOPK * TOPK)
        all_indices = (ix[..., :, None] * NUM_KEYS + iy[..., None, :]).reshape(b, t, HEADS, TOPK * TOPK)
        scores, pk = jax.lax.top_k(all_scores, TOPK)
        indices = jnp.take_along_axis(all_indices, pk, axis=-1)
        down = down_embed[indices]
        up = up_embed[indices]
        w = jnp.einsum('btd,bthkd->bthk', hidden_states, down)
        w = jax.nn.silu(w) * jax.nn.softmax(scores, axis=-1)
        experts_states = jnp.einsum('bthk,bthkd->btd', w, up)
        mlp = jax.nn.silu(hidden_states @ Wg.T) * (hidden_states @ Wu.T) @ Wd.T
        return mlp + experts_states
    x = L0_attn_hidden_states
    mod = (_silu(L0_c) @ L0_wmod).reshape(L0_c.shape[0], 6, 1, -1)
    sa, ca, ga, sb, cb, gb = (mod[:, 0], mod[:, 1], mod[:, 2], mod[:, 3], mod[:, 4], mod[:, 5])
    ga = (2 * (ga >= 0) - 1) * jnp.maximum(jnp.abs(ga), 0.25)
    gb = (2 * (gb >= 0) - 1) * jnp.maximum(jnp.abs(gb), 0.25)
    h = _layernorm(x, axis=-1) * (1 + ca) + sa
    x = x + ga * _L0_attn_ref(h, L0_attn_Wqkv, L0_attn_bqkv, L0_attn_Wd, L0_attn_bd)
    h = _layernorm(x, axis=-1) * (1 + cb) + sb
    x = x + gb * _L0_ffn_ref(h, L0_ffn_Wq, L0_ffn_keys, L0_ffn_down_embed, L0_ffn_up_embed, L0_ffn_Wg, L0_ffn_Wu, L0_ffn_Wd)
    return x

_drawn_inputs = setup_inputs


def setup_inputs(seed=0):
    import zlib

    import numpy as np

    out = dict(_drawn_inputs(seed))
    spreads = {'L0_attn_bqkv': (0.0, 0.1), 'L0_attn_bd': (0.0, 0.355)}
    factors = {'L0_ffn_Wq': 8.0, 'L0_ffn_keys': 8.0, 'L0_ffn_down_embed': 8.0, 'L0_ffn_up_embed': 8.0}
    for name, (base, spread) in spreads.items():
        noise = np.random.default_rng([zlib.crc32(name.encode()), seed]).standard_normal(out[name].shape)
        drawn = base * np.exp(spread * noise) if base else spread * noise
        out[name] = jnp.asarray(drawn.astype(out[name].dtype))
    for name, factor in factors.items():
        out[name] = (out[name] * factor).astype(out[name].dtype)
    return out
```

```python
import concourse.bass as bass
from concourse import mybir
from contextlib import ExitStack

F32 = mybir.dt.float32
BF16 = mybir.dt.bfloat16
U32 = mybir.dt.uint32
ALU = mybir.AluOpType
ACT = mybir.ActivationFunctionType
AX = mybir.AxisListType

B, S, D = 4, 1024, 128
P = 128
NI = S // P
H, HD = 16, 8
G2 = H // 2
SCALE = HD ** -0.5
EPS = 1e-5
INTER, RH, NKEY, NEXP, TOPK = 512, 4, 128, 2048, 8
HALF = 64
NB = 32
NC = P // NB
KR = 48
SLOTS = RH * TOPK + 1
BIG = -1.0e30

C_ID, C_MASK, C_BONES = 0, P, 2 * P
C_COS = C_BONES + H
C_SIN = C_COS + S
C_EYE = C_SIN + S
C_DZ = C_EYE + NB * NB
C_IOTA = C_DZ + HD + 1
C_ALL = C_IOTA + TOPK


def constants():
    import numpy as np
    c = np.zeros((P, C_ALL), np.float32)
    c[:, C_ID:C_ID + P] = np.eye(P)
    c[:, C_MASK:C_MASK + P] = np.triu(np.full((P, P), BIG), 1)
    row = np.arange(P)
    hh, d, g2 = row // 64, row // 8 % 8, row % 8
    c[row, C_BONES + 2 * g2 + hh] = 1.0
    t = np.arange(S, dtype=np.float32)
    cos, sin = np.cos(t), np.sin(t)
    c[:, C_COS:C_COS + S] = np.where(d[:, None] < 2, cos[None], 1.0)
    c[:, C_SIN:C_SIN + S] = np.where(d[:, None] == 0, -sin[None], np.where(d[:, None] == 1, sin[None], 0.0))
    c[:, C_EYE:C_EYE + NB * NB] = np.eye(NB).reshape(1, -1)
    c[:, C_DZ + HD] = 1.0
    c[:, C_IOTA:C_IOTA + TOPK] = np.arange(TOPK)
    return c


def adaln_block(nc, x, wqkv, bqkv, wd, bd, wq, keys, down, up, wg, wu, wd2, cc, wmod, cst_in, out, STOP=3, dbg=None):
    ctx = ExitStack()
    with ctx:
        def sb(name, shape, dt=F32, at=ctx):
            return at.enter_context(nc.sbuf_tensor(name, shape, dt))

        def sem(name):
            return ctx.enter_context(nc.semaphore(name))

        def dram(name, shape, dt):
            return nc.dram_tensor(name, shape, dt, kind="Internal").ap()

        qs_d = dram("qs_d", [B, 2, KR, G2, S], BF16)
        ks_d = dram("ks_d", [B, 2, KR, G2, S], BF16)
        ed_d = dram("ed_d", [B, P, 2, G2, P], F32)
        rd_d = dram("rd_d", [B * H, P], F32)
        z_d = dram("z_d", [P, 2, NB, NB], F32)
        table = dram("table", [NEXP, 2 * D], F32)

        cst = sb("cst", [P, C_ALL])
        xs = sb("xs", [P, B, NI, D])
        mod = sb("mod", [P, B, 6, D])
        wT = sb("wT", [P, 24, D])
        bdrow = sb("bdrow", [1, D])
        ones1 = sb("ones1", [1, P])
        a_all = sb("a_all", [P, B, NI, H, HD + 1])
        ident = cst[:, C_ID:C_ID + P]

        pb = [ctx.enter_context(nc.psum_tensor(f"pb{i}", [P, 1024], F32)) for i in range(4)]

        names = ("w_in", "tab_in", "c_ready", "wt_ps", "wt_sb", "silu_c", "scb", "mod_ps", "mod_sb", "setup_dve", "pool_c",
                 "bias_ps",
                 "h_ready", "hT_ps", "hT_sb", "var_ready", "sd_ready", "proj", "rope", "parts", "parts_st", "prod_ready",
                 "ld_ps", "ld_sb", "v_ps", "v_sb",
                 "ka_free", "qk_ld", "max_lg", "max_red", "mx_ready", "mT_done", "qm_ready", "e_lg", "exp_done",
                 "av_done", "ed_masked", "ast_ready", "r_done", "r_evac", "ed_st", "a_ready",
                 "rd_ready", "rdT_ps", "rdT_sb", "rd_st", "x_ld", "es_ready", "z_ready", "z_st",
                 "vt_ld", "rr_ready", "px_done", "acur", "acc_done",
                 "ac_ready", "at_ps", "at_sb", "y_ps", "h2_ready", "var2", "sd2", "h2T_ps", "h2T_sb", "gu_ps", "sg", "act",
                 "mlp_ps", "q_ps", "q_sb", "sim_ps", "sim_red", "sub_ready", "ex_ready", "idx_ready", "gathered",
                 "dots", "silu_w", "g_free", "out_ready", "out_st", "act_own", "dve", "pool_own", "passed_dve", "passed_pe", "passed_pool")
        s = {n: sem(n) for n in names}

        def link(eng, ins, own, count):
            count[0] += 1
            ins.then_inc(own, 1)
            eng.wait_ge(own, count[0])

        def wait_alone(eng, what, value, passed):
            eng.wait_ge(s[what], value)
            eng.sem_inc(s[passed], 1)

        att = ExitStack()
        v_all = sb("v_all", [P, B, NI, H, HD], at=att)
        ldg = sb("ldg", [P, B, NI, H], at=att)
        ka = sb("ka", [P, G2, S], BF16, at=att)
        qa = sb("qa", [P, G2, P], BF16, at=att)
        mx = sb("mx", [P, G2, P], BF16, at=att)
        identb = sb("identb", [P, P], BF16, at=att)
        maskb = sb("maskb", [P, P], BF16, at=att)
        prep = ExitStack()
        wnat = sb("wnat", [P, 24, D], at=prep)
        wrow = sb("wrow", [1, 3 * D], at=prep)
        brow = sb("brow", [1, 4, P], at=prep)
        wp = sb("wp", [P, 4, P], at=prep)
        bcol = sb("bcol", [P, 4], at=prep)
        cT = sb("cT", [P, B], at=prep)
        sc = sb("sc", [P, B], at=prep)
        scb = sb("scb", [P, B, P], at=prep)
        wm = sb("wm", [P, 6 * D], at=prep)
        tmpm = sb("tmpm", [P, B, D], at=prep)
        st = sb("st", [P, NI, 6], at=prep)
        mv = sb("mv", [P, NI, 2], at=prep)
        sd = sb("sd", [P, NI], at=prep)
        rs = sb("rs", [P, NI], at=prep)
        hn = sb("hn", [P, NI, D], at=prep)
        hT = sb("hT", [P, S], at=prep)
        t1 = sb("t1", [P, S], at=prep)
        t2 = sb("t2", [P, S], at=prep)
        qf = sb("qf", [P, S], at=prep)
        kf = sb("kf", [P, S], at=prep)
        prod = sb("prod", [P, S], at=prep)
        qkp = sb("qkp", [P, 2, 3, S], BF16, at=prep)

        prep.close()
        qm = sb("qm", [P, G2, P], BF16, at=att)
        mraw = sb("mraw", [P, H, 2], at=att)
        mfin = sb("mfin", [P, H], at=att)
        esub = sb("esub", [P, B, H], at=att)
        es = sb("es", [P, B, H], at=att)
        et = sb("et", [P, 2, 8, P], at=att)
        ed = sb("ed", [P, 2, G2, P], at=att)
        ast = sb("ast", [P, NI - 1, H, HD + 1], at=att)
        rsb = sb("rsb", [P, B, H, HD + 1], at=att)
        rdn = sb("rdn", [P, B, H], at=att)
        rn = sb("rn", [P, B, H, HD], at=att)
        rdT = sb("rdT", [B * H, P], at=att)
        xb = sb("xb", [P, 2, NB, NB], at=att)
        rdb = sb("rdb", [P, 2, NB], at=att)
        zb = sb("zb", [P, 2, NB, NB], at=att)
        tb = sb("tb", [P, 2, NB, NB], at=att)
        edb = sb("edb", [P, 2, G2, P], at=att)
        vtb = sb("vtb", [P, H, NB], at=att)
        rr = sb("rr", [P, H, HD], at=att)
        acur = sb("acur", [P, H, HD], at=att)
        att.close()

        ffn = ctx
        gbuf = sb("gbuf", [P, SLOTS, 2 * D], at=ffn)
        pr = sb("pr", [P, SLOTS, D], at=ffn)
        ac = sb("ac", [P, B, H, HD], at=ffn)
        aT = sb("aT", [P, B, P], at=ffn)
        x1 = sb("x1", [P, B, D], at=ffn)
        tf = sb("tf", [P, B, D], at=ffn)
        h2 = sb("h2", [P, B, D], at=ffn)
        h2T = sb("h2T", [P, B, P], at=ffn)
        st2 = sb("st2", [P, B, 6], at=ffn)
        mv2 = sb("mv2", [P, B, 2], at=ffn)
        sd2 = sb("sd2t", [P, B], at=ffn)
        rs2 = sb("rs2", [P, B], at=ffn)
        sg = sb("sgt", [P, 2, 512], at=ffn)
        hid = sb("hid", [P, 4, B, P], at=ffn)
        qT = sb("qT", [P, 4, B, P], at=ffn)
        sv = sb("sv", [P, 2, B, RH, TOPK], at=ffn)
        iv = sb("iv", [P, 2, B, RH, TOPK], U32, at=ffn)
        ivf = sb("ivf", [P, 2, B * RH, TOPK], at=ffn)
        allsc = sb("allsc", [P, B * RH, TOPK, TOPK], at=ffn)
        scs = sb("scs", [P, B * RH, TOPK], at=ffn)
        pos = sb("pos", [P, B * RH, TOPK], U32, at=ffn)
        pab = sb("pab", [P, 2, B * RH * TOPK], U32, at=ffn)
        pabf = sb("pabf", [P, 2, B * RH * TOPK], at=ffn)
        oh = sb("oh", [P, B * RH * TOPK, TOPK], at=ffn)
        isel = sb("isel", [P, 2, B * RH * TOPK], at=ffn)
        ef = sb("ef", [P, B * RH * TOPK], at=ffn)
        ei = sb("ei", [P, B * RH * TOPK], U32, at=ffn)
        wsub = sb("wsub", [P, B * RH, TOPK], at=ffn)
        wex = sb("wex", [P, B * RH, TOPK], at=ffn)
        wsum = sb("wsum", [P, B * RH], at=ffn)
        wrs = sb("wrs", [P, B * RH], at=ffn)
        coef = sb("coef", [P, B, SLOTS], at=ffn)
        wd_s = sb("wd_s", [P, SLOTS], at=ffn)
        ws = sb("ws", [P, SLOTS], at=ffn)
        er = sb("er", [P, D], at=ffn)
        ot = sb("ot", [P, D], at=ffn)
        print("sbuf left", nc.sbuf_bytes_remaining)

        def chunks_before(i):
            return 4 * sum(2 * (j + 1) for j in range(i))

        def chunk(i, b, n):
            return chunks_before(i) + b * (2 * (i + 1)) + n

        def mcount(i):
            return H * (1 if i < 4 else 2)

        def mlg(i, b, n):
            return 4 * sum(mcount(j) for j in range(i)) + b * mcount(i) + n

        def off(i, b, n):
            return 4 * sum(2 * j for j in range(i)) + b * (2 * i) + n

        def blocks(i, n):
            res = []
            for hh in range(2):
                for k in range(4):
                    if n < 2:
                        res.append((hh * 4 + k, 4 * n + k, hh, i))
                    else:
                        m = 4 * (n - 2) + k
                        res.append((hh * 4 + k, m // i, hh, m % i))
            return res

        block = ctx.enter_context(nc.Block())
        NSETUP_IN = [0]

        @block.sync
        def _(sp):
            w = s["w_in"]

            def ld(dst, src):
                sp.dma_start(dst, src).then_inc(w, 16)
                NSETUP_IN[0] += 1
            ld(cst[:, :], cst_in)
            ld(wnat[:, 0:3, :], wqkv.rearrange("(t p) d -> p t d", p=P))
            ld(wnat[:, 3, :], wd)
            ld(wnat[:, 4:8, :], wq.rearrange("(t p) d -> p t d", p=P))
            ld(wnat[:, 8:12, :], wg.rearrange("(t p) d -> p t d", p=P))
            ld(wnat[:, 12:16, :], wu.rearrange("(t p) d -> p t d", p=P))
            ld(wnat[:, 16:20, :], wd2.rearrange("p (t d) -> p t d", d=P))
            kn = wnat[:, 20:24, :].rearrange("k (q m) (e n) -> k q m e n", q=2, e=2)
            for h in range(RH):
                ld(kn[:, :, h // 2, h % 2, :], keys[h])
            ld(wrow[:, :], bqkv.rearrange("(a n) -> a n", a=1))
            ld(bdrow[:, :], bd.rearrange("(a n) -> a n", a=1))
            with nc.allow_non_contiguous_dma(reason="512 elements"):
                ld(cT[:, :], cc.rearrange("b k -> k b"))
            ld(wm[:, :], wmod)
            for b in range(B):
                ld(xs[:, b, :, :], x[b].rearrange("(i p) d -> p i d", p=P))
            sp.dma_start(table[:, 0:D], down).then_inc(s["tab_in"], 16)
            sp.dma_start(table[:, D:2 * D], up).then_inc(s["tab_in"], 16)
            with sp.Fori(0, B) as b:
                for qk, dst, order in ((0, qs_d, (0, 0, 1, 1, 0, 2)), (1, ks_d, (0, 1, 0, 1, 2, 0))):
                    sp.wait_ge(s["parts"], 2 * b + qk + 1)
                    for hh in range(2):
                        for r, part in enumerate(order):
                            sp.dma_start(dst[b, hh, r * HD:(r + 1) * HD, :, :].rearrange("d g s -> (d g) s"),
                                         qkp[64 * hh:64 * hh + 64, qk, part, :]).then_inc(s["parts_st"], 16)
            sp.wait_ge(s["parts_st"], 16 * 24 * B)
            if STOP < 2:
                return
            sp.wait_ge(s["pool_c"], 1)
            sp.sem_inc(s["ed_st"], 16)
            for i in range(NI):
                with sp.Fori(0, B) as b:
                    step = 4 * i + b
                    sp.wait_ge(s["ka_free"], step + 1)
                    for hh in range(2):
                        sp.dma_start(ka[64 * hh:64 * hh + KR, :, 0:(i + 1) * P], ks_d[b, hh, :, :, 0:(i + 1) * P]).then_inc(s["qk_ld"], 16)
                        sp.dma_start(qa[64 * hh:64 * hh + KR, :, :], qs_d[b, hh, :, :, i * P:(i + 1) * P]).then_inc(s["qk_ld"], 16)
                    sp.wait_ge(s["ed_masked"], step + 1)
                    sp.dma_start(ed_d[b], ed[:, :, :, :]).then_inc(s["ed_st"], 16)
                sp.wait_ge(s["ed_st"], 64 * (i + 1) + 16)
                sp.wait_ge(s["z_st"], 16 * i) if i else None
                for b in range(B):
                    for c in range(NC):
                        for hh in range(2):
                            sp.dma_start(xb[b * 32 + c * 8:b * 32 + c * 8 + 8, hh, :, :],
                                         ed_d[b, c * NB:(c + 1) * NB, hh, :, c * NB:(c + 1) * NB].rearrange("j g i -> g j i")
                                         ).then_inc(s["x_ld"], 16)
                sp.wait_ge(s["rdT_sb"], i + 1)
                sp.dma_start(rd_d, rdT[:, :]).then_inc(s["rd_st"], 16)
                sp.wait_ge(s["rd_st"], 16 * (i + 1))
                rv = rd_d.rearrange("(b g e) n -> b e g n", b=B, e=2)
                for b in range(B):
                    for c in range(NC):
                        for hh in range(2):
                            sp.dma_start(rdb[b * 32 + c * 8:b * 32 + c * 8 + 8, hh, :], rv[b, hh, :, c * NB:(c + 1) * NB]).then_inc(s["x_ld"], 16)
                sp.wait_ge(s["z_ready"], i + 1)
                sp.dma_start(z_d, zb[:, :, :, :]).then_inc(s["z_st"], 16)
                sp.wait_ge(s["z_st"], 16 * (i + 1))
                with sp.Fori(0, B) as b:
                    sp.wait_ge(s["a_ready"], 4 * i + b + 1)
                    sp.dma_start(edb[:, :, :, :], ed_d[b]).then_inc(s["vt_ld"], 16)
                    zv = z_d.rearrange("(b c g) e k i -> b c e k g i", b=B, c=NC)
                    vv = vtb[:, :, :].rearrange("p (g e) i -> p e g i", e=2)
                    for c in range(NC):
                        for hh in range(2):
                            sp.dma_start(vv[c * NB:(c + 1) * NB, hh, :, :], zv[b, c, hh, :, :, :]).then_inc(s["vt_ld"], 16)
            if STOP < 3:
                return
            sp.wait_ge(s["tab_in"], 32)
            sp.wait_ge(s["pool_c"], 2)
            sp.dma_start(gbuf[:, SLOTS - 1, :], table[NEXP - 1:NEXP, :].broadcast_to([P, 2 * D])).then_inc(s["tab_in"], 16)
            with sp.Fori(0, NI) as i:
                for t in range(B):
                    sp.wait_ge(s["out_ready"], 4 * i + t + 1)
                    sp.dma_start(out[t, bass.ds(i * P, P), :], ot[:, :]).then_inc(s["out_st"], 16)
            sp.wait_ge(s["out_st"], 16 * B * NI)

        @block.gpsimd
        def _(g):
            nc.gpsimd.memset(ones1[:, :], 1.0).then_inc(s["c_ready"], 1)
            nc.gpsimd.memset(ka[:, :, :], 1.0).then_inc(s["c_ready"], 1)
            nc.gpsimd.memset(qa[:, :, :], 0.0).then_inc(s["c_ready"], 1)
            nc.gpsimd.memset(mx[:, :, :], 0.0).then_inc(s["c_ready"], 1)
            nc.gpsimd.memset(a_all[:, :, :, :, :], 1.0).then_inc(s["c_ready"], 1)
            g.wait_ge(s["c_ready"], 5)
            g.sem_inc(s["pool_c"], 1)
            zero = g.to_reg(0.0)
            last_gathered = g.to_reg(NEXP - 2)
            if STOP < 2:
                return
            for i in range(NI):
                with g.Fori(0, B) as b:
                    step = 4 * i + b
                    if i:
                        g.wait_ge(s["a_ready"], 4 * i + 1)
                        g.wait_ge(s["r_done"], step)
                        nc.gpsimd.tensor_copy(ast[:, 0:i, :, :], a_all[:, b, 0:i, :, :]).then_inc(s["ast_ready"], 1)
                    wait_alone(g, "exp_done", chunk(i, b, 1) + 1 + 2, "passed_pool")
                    nc.gpsimd.affine_select(out=ed[:, :, :, :], in_=ed[:, :, :, :], compare_op=ALU.is_ge, fill=zero, base=0,
                                            pattern=[[0, 2], [0, G2], [1, P]], channel_multiplier=-1).then_inc(s["ed_masked"], 1)
            if STOP < 3:
                return
            g.wait_ge(s["a_ready"], 4 * NI + 1)
            nc.gpsimd.memset(gbuf[:, :, :], 0.0).then_inc(s["pool_own"], 1)
            g.wait_ge(s["pool_own"], 1)
            g.sem_inc(s["pool_c"], 1)
            g.wait_ge(s["tab_in"], 48)
            with g.Fori(0, NI) as i:
                g.wait_ge(s["at_ps"], i + 1)
                nc.gpsimd.tensor_copy(ac[:, :, :, :], a_all[:, :, i, :, 0:HD]).then_inc(s["ac_ready"], 1)
                wait_alone(g, "idx_ready", i + 1, "passed_pool")
                for t in range(B):
                    wait_alone(g, "g_free", 4 * i + t + 1, "passed_pool")
                    for k in range(SLOTS - 1):
                        nc.gpsimd.indirect_dma_start(gbuf[:, k, :], None, table,
                                                     bass.IndirectOffsetOnAxis(ei[:, t * 32 + k:t * 32 + k + 1], 0),
                                                     bounds_check=last_gathered, oob_is_err=False).then_inc(s["gathered"], 16)

        @block.scalar
        def _(a):
            a.wait_ge(s["w_in"], 16 * NSETUP_IN[0])
            nc.scalar.activation(sc[:, :], cT[:, :], ACT.Silu).then_inc(s["silu_c"], 1)
            for n in range(6):
                a.wait_ge(s["wt_ps"], n + 1)
                nc.scalar.activation(wT[:, 4 * n:4 * n + 4, :], pb[n % 4][:, 0:512].rearrange("p (t d) -> p t d", d=D), ACT.Copy).then_inc(s["wt_sb"], 1)
            with a.Fori(0, B) as b:
                a.wait_ge(s["var_ready"], b + 1)
                nc.scalar.activation(sd[:, :], rs[:, :], ACT.Sqrt).then_inc(s["sd_ready"], 1)
                a.wait_ge(s["hT_ps"], b + 1)
                nc.scalar.activation(hT[:, :], pb[0][:, :], ACT.Copy).then_inc(s["hT_sb"], 1)
                a.wait_ge(s["v_ps"], b + 1)
                nc.scalar.activation(v_all[:, b, :, :, :].rearrange("p i h d -> p (i h d)"), pb[0][:, :], ACT.Copy).then_inc(s["v_sb"], 1)
                a.wait_ge(s["ld_ps"], b + 1)
                nc.scalar.activation(ldg[:, b, :, :].rearrange("p i h -> p (i h)"), pb[3][:, 0:NI * H], ACT.Copy).then_inc(s["ld_sb"], 1)
            if STOP < 2:
                return
            a.sem_inc(s["exp_done"], 2)
            for i in range(NI):
                with a.Fori(0, B) as b:
                    step = 4 * i + b
                    for n in range(2 * (i + 1)):
                        a.wait_ge(s["e_lg"], chunk(i, b, n) + 1)
                        src = pb[1 + n % 2][:, :].rearrange("p (e k i) -> p e k i", e=2, k=4)
                        if n < 2:
                            if n == 0:
                                a.wait_ge(s["ed_st"], 16 * (step + 1))
                            dst = ed[:, :, 4 * n:4 * n + 4, :]
                        else:
                            a.wait_ge(s["av_done"], off(i, b, n - 2) + 1)
                            dst = et[:, n % 2, :, :].rearrange("p (e k) i -> p e k i", e=2)
                        nc.scalar.activation(dst, src, ACT.Exp, scale=SCALE).then_inc(s["exp_done"], 1)
                a.wait_ge(s["mx_ready"], 4 * (i + 1))
                nc.scalar.activation(es[:, :, :], esub[:, :, :], ACT.Exp, scale=SCALE).then_inc(s["es_ready"], 1)
            if STOP < 3:
                return
            with a.Fori(0, NI) as i:
                a.wait_ge(s["at_ps"], i + 2)
                nc.scalar.activation(aT[:, :, :].rearrange("p b n -> p (b n)"), pb[0][:, 0:512], ACT.Copy).then_inc(s["at_sb"], 1)
                a.wait_ge(s["var2"], i + 1)
                nc.scalar.activation(sd2[:, :], rs2[:, :], ACT.Sqrt).then_inc(s["sd2"], 1)
                a.wait_ge(s["h2T_ps"], i + 1)
                nc.scalar.activation(h2T[:, :, :].rearrange("p b n -> p (b n)"), pb[0][:, 0:512], ACT.Copy).then_inc(s["h2T_sb"], 1)
                for c in range(4):
                    a.wait_ge(s["gu_ps"], 4 * i + c + 1)
                    if c >= 2:
                        a.wait_ge(s["act"], 4 * i + c - 1)
                    nc.scalar.activation(sg[:, c % 2, :], pb[1 + c % 2][:, 0:512], ACT.Silu).then_inc(s["sg"], 1)
                for c in range(4):
                    a.wait_ge(s["q_ps"], 4 * i + c + 1)
                    nc.scalar.activation(qT[:, c, :, :].rearrange("p b n -> p (b n)"), pb[0][:, (c % 2) * 512:(c % 2) * 512 + 512], ACT.Copy).then_inc(s["q_sb"], 1)
                a.wait_ge(s["sub_ready"], i + 1)
                nc.scalar.activation(wex[:, :, :], wsub[:, :, :], ACT.Exp).then_inc(s["ex_ready"], 1)
                for t in range(B):
                    a.wait_ge(s["dots"], 4 * i + t + 1)
                    nc.scalar.activation(ws[:, :], wd_s[:, :], ACT.Silu).then_inc(s["silu_w"], 1)

        @block.tensor
        def _(pe):
            mm = nc.tensor.matmul
            pe.wait_ge(s["w_in"], 16 * NSETUP_IN[0])
            for n in range(6):
                if n >= 4:
                    pe.wait_ge(s["wt_sb"], n - 3)
                for t in range(4):
                    last = mm(pb[n % 4][:, t * P:(t + 1) * P], wnat[:, 4 * n + t, :], ident, start=True, stop=True)
                last.then_inc(s["wt_ps"], 1)
            pe.wait_ge(s["scb"], 1)
            pe.wait_ge(s["wt_sb"], 6)
            for b in range(B):
                if b:
                    pe.wait_ge(s["mod_sb"], b)
                mm(pb[0][:, 0:512], scb[:, b, :], wm[:, 0:512], start=True, stop=True)
                mm(pb[0][:, 512:768], scb[:, b, :], wm[:, 512:768], start=True, stop=True).then_inc(s["mod_ps"], 1)
            pe.wait_ge(s["c_ready"], 5)
            pe.wait_ge(s["setup_dve"], 1)
            for n in range(4):
                last = mm(pb[3][:, n:n + 1], brow[0:1, n, :], ones1[0:1, 0:1], start=True, stop=True)
            last.then_inc(s["bias_ps"], 1)
            with pe.Fori(0, B) as b:
                pe.wait_ge(s["h_ready"], b + 1)
                for t in range(NI):
                    last = mm(pb[0][:, t * P:(t + 1) * P], hn[:, t, :], ident, start=True, stop=True)
                last.then_inc(s["hT_ps"], 1)
                pe.wait_ge(s["hT_sb"], b + 1)
                for t in range(NI):
                    mm(pb[0][:, t * P:(t + 1) * P], hT[:, t * P:(t + 1) * P], wT[:, 2, :], start=True, stop=False)
                    last = mm(pb[0][:, t * P:(t + 1) * P], ones1[0:1, :], wrow[0:1, 2 * D:3 * D], start=False, stop=True)
                last.then_inc(s["v_ps"], 1)
                for qk in range(2):
                    if qk:
                        pe.wait_ge(s["rope"], 2 * b + 1)
                    for w in range(2):
                        for half in range(2):
                            last = mm(pb[1 + w][:, half * 512:(half + 1) * 512], wp[:, 2 * qk + w, :], hT[:, half * 512:(half + 1) * 512], start=True, stop=True)
                    last.then_inc(s["proj"], 1)
                pe.wait_ge(s["prod_ready"], b + 1)
                for t in range(NI):
                    last = mm(pb[3][:, t * H:(t + 1) * H], prod[:, t * P:(t + 1) * P], cst[:, C_BONES:C_BONES + H], start=True, stop=True)
                last.then_inc(s["ld_ps"], 1)
                pe.wait_ge(s["v_sb"], b + 1)
                pe.wait_ge(s["ld_sb"], b + 1)
            pe.sem_inc(s["av_done"], 2)
            pe.sem_inc(s["ka_free"], 1)
            if STOP < 2:
                return
            rp = pb[3][:, 0:H * (HD + 1)].rearrange("p (h d) -> p h d", h=H)
            px = pb[3][:, 512:640].rearrange("p (h d) -> p h d", h=H)
            pacc = pb[3][:, 640:768].rearrange("p (h d) -> p h d", h=H)
            for i in range(NI):
                with pe.Fori(0, B) as b:
                    step = 4 * i + b
                    pe.wait_ge(s["qk_ld"], 64 * (step + 1))
                    n = 0
                    for h in range(H):
                        g2, hh = h // 2, h % 2
                        for c0 in range(0, (i + 1) * P, 512):
                            c1 = min(c0 + 512, (i + 1) * P)
                            bank = pb[0][:, (n % 2) * 512:(n % 2) * 512 + 512]
                            if n >= 2:
                                pe.wait_ge(s["max_red"], mlg(i, b, n - 1))
                            last = mm(bank[:, 0:c1 - c0], qa[64 * hh:64 * hh + KR, g2, :], ka[64 * hh:64 * hh + KR, g2, c0:c1],
                                      start=True, stop=c1 < (i + 1) * P)
                            if c1 == (i + 1) * P:
                                last = mm(bank[:, i * P - c0:i * P - c0 + P], identb[:, :], maskb[:, :], start=False, stop=True)
                            last.then_inc(s["max_lg"], 1)
                            n += 1
                    pe.wait_ge(s["mx_ready"], step + 1)
                    for g2 in range(G2):
                        last = mm(pb[0][:, g2 * P:(g2 + 1) * P], mx[:, g2, :], identb[:, :], start=True, stop=True)
                    last.then_inc(s["mT_done"], 1)
                    pe.wait_ge(s["qm_ready"], step + 1)
                    if i:
                        pe.wait_ge(s["ast_ready"], 4 * (i - 1) + b + 1)
                        pe.wait_ge(s["r_evac"], step)
                    started = [False]

                    def multiply(n):
                        if n >= 2:
                            pe.wait_ge(s["exp_done"], chunk(i, b, n) + 3)
                        else:
                            pe.wait_ge(s["ed_masked"], step + 1)
                        for k, g2, hh, j in blocks(i, n):
                            h = 2 * g2 + hh
                            lhs = et[:, n % 2, k, :] if n >= 2 else ed[:, hh, g2, :]
                            rhs = ast[:, j, h, :] if n >= 2 else cst[:, C_DZ:C_DZ + HD + 1]
                            last = mm(rp[:, h, :], lhs, rhs, start=not started[0], stop=True, skip_group_check=True)
                            started[0] = True
                        return last
                    total = 2 * (i + 1)
                    for n in range(total):
                        pe.wait_ge(s["exp_done"], chunk(i, b, n) + 1)
                        for k, g2, hh, j in blocks(i, n):
                            last = mm(pb[1 + n % 2][:, k * P:(k + 1) * P], ka[64 * hh:64 * hh + KR + 2, g2, j * P:(j + 1) * P],
                                      qm[64 * hh:64 * hh + KR + 2, g2, :], start=True, stop=True)
                        last.then_inc(s["e_lg"], 1)
                        if n >= 3:
                            multiply(n - 1).then_inc(s["av_done"], 1)
                    if total > 2:
                        multiply(total - 1).then_inc(s["av_done"], 1)
                    multiply(0)
                    multiply(1).then_inc(s["r_done"], 1)
                    pe.wait_ge(s["r_done"], step + 1)
                    pe.sem_inc(s["ka_free"], 1)
                pe.wait_ge(s["rd_ready"], i + 1)
                mm(pb[0][0:B * H, 0:P], rdn[:, :, :].rearrange("p b h -> p (b h)"), ident, start=True, stop=True).then_inc(s["rdT_ps"], 1)
                with pe.Fori(0, B) as b:
                    step = 4 * i + b
                    pe.wait_ge(s["vt_ld"], 16 * 9 * (step + 1))
                    for c in range(NC):
                        wait_alone(pe, "rr_ready", 4 * step + c + 1, "passed_pe")
                        rows = slice(c * NB, (c + 1) * NB)
                        for h in range(H):
                            last = mm(px[rows, h, :], vtb[rows, h, :], rr[rows, h, :], start=True, stop=True, skip_group_check=True)
                        last.then_inc(s["px_done"], 1)
                        if c < NC - 1:
                            pe.wait_ge(s["acur"], 4 * step + c + 1)
                            for h in range(H):
                                last = mm(pacc[:, h, :], edb[rows, h % 2, h // 2, :], acur[rows, h, :], start=(c == 0 and h == 0), stop=True, skip_group_check=True)
                            last.then_inc(s["acc_done"], 1)
            if STOP < 3:
                return
            pe.sem_inc(s["at_ps"], 1)
            with pe.Fori(0, NI) as i:
                pe.wait_ge(s["ac_ready"], i + 1)
                for t in range(B):
                    last = mm(pb[0][:, t * P:(t + 1) * P], ac[:, t, :, :].rearrange("p h d -> p (h d)"), ident, start=True, stop=True)
                last.then_inc(s["at_ps"], 1)
                pe.wait_ge(s["at_sb"], i + 1)
                for t in range(B):
                    mm(pb[0][:, 512 + t * P:512 + (t + 1) * P], aT[:, t, :], wT[:, 3, :], start=True, stop=False)
                    last = mm(pb[0][:, 512 + t * P:512 + (t + 1) * P], ones1[0:1, :], bdrow[0:1, :], start=False, stop=True)
                last.then_inc(s["y_ps"], 1)
                pe.wait_ge(s["h2_ready"], i + 1)
                for t in range(B):
                    last = mm(pb[0][:, t * P:(t + 1) * P], h2[:, t, :], ident, start=True, stop=True)
                last.then_inc(s["h2T_ps"], 1)
                pe.wait_ge(s["h2T_sb"], i + 1)
                hx = h2T[:, :, :].rearrange("p b n -> p (b n)")
                for c in range(4):
                    if c >= 2:
                        pe.wait_ge(s["act"], 4 * i + c - 1)
                    mm(pb[1 + c % 2][:, 0:512], wT[:, 8 + c, :], hx, start=True, stop=True)
                    mm(pb[1 + c % 2][:, 512:1024], wT[:, 12 + c, :], hx, start=True, stop=True).then_inc(s["gu_ps"], 1)
                for c in range(4):
                    if c >= 2:
                        pe.wait_ge(s["q_sb"], 4 * i + c - 1)
                    mm(pb[0][:, (c % 2) * 512:(c % 2) * 512 + 512], wT[:, 4 + c, :], hx, start=True, stop=True).then_inc(s["q_ps"], 1)
                pe.wait_ge(s["act"], 4 * i + 4)
                for t in range(B):
                    for c in range(4):
                        last = mm(pb[3][:, t * P:(t + 1) * P], hid[:, c, t, :], wT[:, 16 + c, :], start=c == 0, stop=c == 3)
                last.then_inc(s["mlp_ps"], 1)
                pe.wait_ge(s["q_sb"], 4 * i + 4)
                for t in range(B):
                    if t >= 2:
                        pe.wait_ge(s["sim_red"], 4 * i + t - 1)
                    for q in range(2):
                        for h in range(RH):
                            c, e = 2 * q + h // 2, h % 2
                            last = mm(pb[1 + t % 2][:, e * 512 + c * P:e * 512 + (c + 1) * P], qT[64 * e:64 * e + 64, c, t, :],
                                      wT[64 * e:64 * e + 64, 20 + c, :], start=True, stop=True)
                    last.then_inc(s["sim_ps"], 1)
                pe.wait_ge(s["out_ready"], 4 * i + 4)

        @block.vector
        def _(v):
            V = nc.vector
            n = [0]

            def lk(ins):
                link(v, ins, s["dve"], n)

            def restart():
                v.sem_clear(s["dve"])
                n[0] = 0
            v.wait_ge(s["w_in"], 16 * NSETUP_IN[0])
            v.wait_ge(s["c_ready"], 5)
            V.tensor_copy(identb[:, :], ident)
            lk(V.tensor_copy(maskb[:, :], cst[:, C_MASK:C_MASK + P]))
            v.wait_ge(s["wt_sb"], 1)
            for qk in range(2):
                src = wT[:, qk, :].rearrange("p (g e d) -> p e d g", g=G2, e=2)
                bsrc = wrow[0:1, qk * D:(qk + 1) * D].rearrange("p (g e d) -> p e d g", g=G2, e=2)
                for w in range(2):
                    dst = wp[:, 2 * qk + w, :].rearrange("p (e d g) -> p e d g", e=2, g=G2)
                    bdst = brow[0:1, 2 * qk + w, :].rearrange("p (e d g) -> p e d g", e=2, g=G2)
                    for dd, ss in ((dst, src), (bdst, bsrc)):
                        for e in range(2):
                            if w == 0:
                                lk(V.tensor_copy(dd[:, e], ss[:, e]))
                            else:
                                lk(V.tensor_copy(dd[:, e, 2:8], ss[:, e, 2:8]))
                                lk(V.tensor_copy(dd[:, e, 0], ss[:, e, 1]))
                                lk(V.tensor_copy(dd[:, e, 1], ss[:, e, 0]))
            v.sem_inc(s["setup_dve"], 1)
            v.wait_ge(s["silu_c"], 1)
            V.tensor_copy(scb[:, :, :], sc[:, :].unsqueeze(2).broadcast_to([P, B, P])).then_inc(s["scb"], 1)
            for b in range(B):
                v.wait_ge(s["mod_ps"], b + 1)
                V.tensor_copy(mod[:, b, :, :].rearrange("p m d -> p (m d)"), pb[0][:, 0:768]).then_inc(s["mod_sb"], 1)
            v.wait_ge(s["mod_sb"], B)
            for m in (1, 4):
                lk(V.tensor_scalar(mod[:, :, m, :], mod[:, :, m, :], 1.0, None, ALU.add))
            for m in (2, 5):
                lk(V.tensor_scalar(tmpm[:, :, :], mod[:, :, m, :], -1.0, 0.25, ALU.mult, ALU.max))
                lk(V.tensor_tensor(tmpm[:, :, :], tmpm[:, :, :], mod[:, :, m, :], ALU.max))
                lk(V.tensor_scalar(mod[:, :, m, :], mod[:, :, m, :], 0.0, 2.0, ALU.is_ge, ALU.mult))
                lk(V.tensor_scalar(mod[:, :, m, :], mod[:, :, m, :], -1.0, None, ALU.add))
                lk(V.tensor_tensor(mod[:, :, m, :], mod[:, :, m, :], tmpm[:, :, :], ALU.mult))
            v.wait_ge(s["bias_ps"], 1)
            lk(V.tensor_copy(bcol[:, :], pb[3][:, 0:4]))
            with v.Fori(0, B) as b:
                restart()
                for t in range(NI):
                    V.bn_stats(st[:, t, :], xs[:, b, t, :]).then_inc(s["dve"], 1)
                n[0] += NI
                v.wait_ge(s["dve"], n[0])
                for t in range(NI):
                    V.bn_aggr(mv[:, t, :], st[:, t, :]).then_inc(s["dve"], 1)
                n[0] += NI
                v.wait_ge(s["dve"], n[0])
                V.tensor_scalar(rs[:, :], mv[:, :, 1], EPS, None, ALU.add).then_inc(s["var_ready"], 1)
                v.wait_ge(s["sd_ready"], b + 1)
                lk(V.reciprocal(rs[:, :], sd[:, :]))
                for t in range(NI):
                    V.tensor_scalar(hn[:, t, :], xs[:, b, t, :], mv[:, t, 0:1], rs[:, t:t + 1], ALU.subtract, ALU.mult).then_inc(s["dve"], 1)
                n[0] += NI
                v.wait_ge(s["dve"], n[0])
                lk(V.tensor_tensor(hn[:, :, :], hn[:, :, :], mod[:, b, 1:2, :].broadcast_to([P, NI, D]), ALU.mult))
                V.tensor_tensor(hn[:, :, :], hn[:, :, :], mod[:, b, 0:1, :].broadcast_to([P, NI, D]), ALU.add).then_inc(s["h_ready"], 1)
                for qk, res in ((0, qf), (1, kf)):
                    v.wait_ge(s["proj"], 2 * b + qk + 1)
                    V.scalar_tensor_tensor(t1[:, :], pb[1][:, :], bcol[:, 2 * qk:2 * qk + 1], cst[:, C_COS:C_COS + S], ALU.add, ALU.mult).then_inc(s["dve"], 1)
                    V.scalar_tensor_tensor(t2[:, :], pb[2][:, :], bcol[:, 2 * qk + 1:2 * qk + 2], cst[:, C_SIN:C_SIN + S], ALU.add, ALU.mult).then_inc(s["dve"], 1)
                    n[0] += 2
                    v.wait_ge(s["dve"], n[0])
                    lk(V.tensor_tensor(res[:, :], t1[:, :], t2[:, :], ALU.add))
                    v.sem_inc(s["rope"], 1)
                    lk(V.tensor_copy(qkp[:, qk, 0, :], res[:, :]))
                    lk(V.tensor_tensor(t1[:, :], res[:, :], qkp[:, qk, 0, :], ALU.subtract))
                    lk(V.tensor_copy(qkp[:, qk, 1, :], t1[:, :]))
                    V.tensor_tensor(qkp[:, qk, 2, :], t1[:, :], qkp[:, qk, 1, :], ALU.subtract).then_inc(s["parts"], 1)
                    v.wait_ge(s["parts"], 2 * b + qk + 1)
                V.tensor_tensor(prod[:, :], qf[:, :], kf[:, :], ALU.mult).then_inc(s["prod_ready"], 1)
                v.wait_ge(s["ld_ps"], b + 1)
                v.wait_ge(s["parts_st"], 16 * 24 * (b + 1))
            if STOP < 2:
                return
            rp = pb[3][:, 0:H * (HD + 1)].rearrange("p (h d) -> p h d", h=H)
            px = pb[3][:, 512:640].rearrange("p (h d) -> p h d", h=H)
            pacc = pb[3][:, 640:768].rearrange("p (h d) -> p h d", h=H)
            v.sem_inc(s["a_ready"], 1)
            mrow = mx[:, :, :].rearrange("p g (e c) -> p g e c", e=2)
            for i in range(NI):
                with v.Fori(0, B) as b:
                    step = 4 * i + b
                    restart()
                    k = 0
                    nch = 1 if i < 4 else 2
                    for h in range(H):
                        for c in range(nch):
                            w = min(512, (i + 1) * P - 512 * c)
                            v.wait_ge(s["max_lg"], mlg(i, b, k) + 1)
                            V.reduce_max(mraw[:, h, c:c + 1], pb[0][:, (k % 2) * 512:(k % 2) * 512 + w], AX.X).then_inc(s["max_red"], 1)
                            k += 1
                    v.wait_ge(s["max_red"], mlg(i, b, k))
                    if nch == 2:
                        lk(V.tensor_tensor(mfin[:, :], mraw[:, :, 0], mraw[:, :, 1], ALU.max))
                    else:
                        lk(V.tensor_copy(mfin[:, :], mraw[:, :, 0]))
                    mf = mfin[:, :].rearrange("p (g e) -> p g e", e=2)
                    lk(V.tensor_scalar(mrow[:, :, :, KR], mf, -1.0, None, ALU.mult))
                    lk(V.scalar_tensor_tensor(mrow[:, :, :, KR + 1], mf, -1.0, mrow[:, :, :, KR], ALU.mult, ALU.subtract))
                    eb = esub[:, b, :].rearrange("p (g e) -> p g e", e=2)
                    lb = ldg[:, b, i, :].rearrange("p (g e) -> p g e", e=2)
                    if i:
                        v.wait_ge(s["es_ready"], i)
                    lk(V.tensor_tensor(eb, lb, mrow[:, :, :, KR], ALU.add))
                    V.tensor_tensor(eb, eb, mrow[:, :, :, KR + 1], ALU.add).then_inc(s["mx_ready"], 1)
                    v.wait_ge(s["mT_done"], step + 1)
                    V.tensor_tensor(qm[:, :, :].rearrange("p g n -> p (g n)"), qa[:, :, :].rearrange("p g n -> p (g n)"), pb[0][:, :], ALU.add).then_inc(s["qm_ready"], 1)
                    v.wait_ge(s["r_done"], step + 1)
                    V.tensor_copy(rsb[:, b, :, :], rp).then_inc(s["r_evac"], 1)
                restart()
                v.wait_ge(s["r_evac"], 4 * (i + 1))
                V.reciprocal(rdn[:, :, :], rsb[:, :, :, HD]).then_inc(s["rd_ready"], 1)
                v.wait_ge(s["es_ready"], i + 1)
                v.wait_ge(s["rd_ready"], i + 1)
                lk(V.tensor_tensor(rn[:, :, :, :], v_all[:, :, i, :, :], es[:, :, :].unsqueeze(3).broadcast_to([P, B, H, HD]), ALU.mult))
                lk(V.tensor_tensor(rn[:, :, :, :], rn[:, :, :, :], rsb[:, :, :, 0:HD], ALU.add))
                lk(V.tensor_tensor(rn[:, :, :, :], rn[:, :, :, :], rdn[:, :, :].unsqueeze(3).broadcast_to([P, B, H, HD]), ALU.mult))
                v.wait_ge(s["rdT_ps"], i + 1)
                V.tensor_copy(rdT[:, :], pb[0][0:B * H, 0:P]).then_inc(s["rdT_sb"], 1)
                v.wait_ge(s["z_st"], 16 * i) if i else None
                for e in range(2):
                    lk(V.tensor_copy(zb[:, e, :, :].rearrange("p k i -> p (k i)"), cst[:, C_EYE:C_EYE + NB * NB]))
                v.wait_ge(s["x_ld"], 16 * 64 * (i + 1))
                lk(V.tensor_tensor(xb[:, :, :, :], xb[:, :, :, :], rdb[:, :, :].unsqueeze(2).broadcast_to([P, 2, NB, NB]), ALU.mult))
                for j in range(NB - 1):
                    w, u = NB - 1 - j, j + 1
                    for e in range(2):
                        lk(V.tensor_tensor(tb[:, e, 0:u, 0:w], xb[:, e, j:j + 1, u:].broadcast_to([P, u, w]),
                                           zb[:, e, 0:u, j:j + 1].broadcast_to([P, u, w]), ALU.mult)) if e else \
                            V.tensor_tensor(tb[:, e, 0:u, 0:w], xb[:, e, j:j + 1, u:].broadcast_to([P, u, w]),
                                            zb[:, e, 0:u, j:j + 1].broadcast_to([P, u, w]), ALU.mult)
                    ins = V.tensor_tensor(zb[:, :, 0:u, u:], zb[:, :, 0:u, u:], tb[:, :, 0:u, 0:w], ALU.add)
                    if j < NB - 2:
                        lk(ins)
                    else:
                        ins.then_inc(s["z_ready"], 1)
                with v.Fori(0, B) as b:
                    step = 4 * i + b
                    restart()
                    for c in range(NC):
                        rows = slice(c * NB, (c + 1) * NB)
                        if c == 0:
                            V.tensor_copy(rr[rows, :, :], rn[rows, b, :, :]).then_inc(s["rr_ready"], 1)
                        else:
                            v.wait_ge(s["acc_done"], 3 * step + c)
                            lk(V.tensor_tensor(rr[rows, :, :], pacc[rows, :, :], rdn[rows, b, :].unsqueeze(2).broadcast_to([NB, H, HD]), ALU.mult))
                            V.tensor_tensor(rr[rows, :, :], rr[rows, :, :], rn[rows, b, :, :], ALU.add).then_inc(s["rr_ready"], 1)
                        v.wait_ge(s["px_done"], 4 * step + c + 1)
                        V.tensor_copy(acur[rows, :, :], px[rows, :, :]).then_inc(s["acur"], 1)
                    v.wait_ge(s["acur"], 4 * step + 4)
                    V.tensor_copy(a_all[:, b, i, :, 0:HD], acur[:, :, :]).then_inc(s["a_ready"], 1)
                    v.wait_ge(s["a_ready"], step + 2)
            if STOP < 3:
                return
            v.sem_inc(s["g_free"], 1)
            with v.Fori(0, NI) as i:
                restart()
                v.wait_ge(s["y_ps"], i + 1)
                lk(V.tensor_tensor(tf[:, :, :].rearrange("p b d -> p b d"), pb[0][:, 512:1024].rearrange("p (b d) -> p b d", b=B), mod[:, :, 2, :], ALU.mult))
                lk(V.tensor_tensor(x1[:, :, :], xs[:, :, i, :], tf[:, :, :], ALU.add))
                for t in range(B):
                    V.bn_stats(st2[:, t, :], x1[:, t, :]).then_inc(s["dve"], 1)
                n[0] += B
                v.wait_ge(s["dve"], n[0])
                for t in range(B):
                    V.bn_aggr(mv2[:, t, :], st2[:, t, :]).then_inc(s["dve"], 1)
                n[0] += B
                v.wait_ge(s["dve"], n[0])
                V.tensor_scalar(rs2[:, :], mv2[:, :, 1], EPS, None, ALU.add).then_inc(s["var2"], 1)
                v.wait_ge(s["sd2"], i + 1)
                lk(V.reciprocal(rs2[:, :], sd2[:, :]))
                for t in range(B):
                    V.tensor_scalar(h2[:, t, :], x1[:, t, :], mv2[:, t, 0:1], rs2[:, t:t + 1], ALU.subtract, ALU.mult).then_inc(s["dve"], 1)
                n[0] += B
                v.wait_ge(s["dve"], n[0])
                lk(V.tensor_tensor(h2[:, :, :], h2[:, :, :], mod[:, :, 4, :], ALU.mult))
                V.tensor_tensor(h2[:, :, :], h2[:, :, :], mod[:, :, 3, :], ALU.add).then_inc(s["h2_ready"], 1)
                for c in range(4):
                    v.wait_ge(s["sg"], 4 * i + c + 1)
                    V.tensor_tensor(hid[:, c, :, :].rearrange("p b n -> p (b n)"), sg[:, c % 2, :], pb[1 + c % 2][:, 512:1024], ALU.mult).then_inc(s["act"], 1)
                for t in range(B):
                    wait_alone(v, "sim_ps", 4 * i + t + 1, "passed_dve")
                    for q in range(2):
                        for h in range(RH):
                            c, e = 2 * q + h // 2, h % 2
                            V.max(sv[:, q, t, h, :], pb[1 + t % 2][:, e * 512 + c * P:e * 512 + (c + 1) * P]).then_inc(s["dve"], 1)
                    n[0] += 8
                    v.wait_ge(s["dve"], n[0])
                    for q in range(2):
                        for h in range(RH):
                            c, e = 2 * q + h // 2, h % 2
                            last = V.max_index(iv[:, q, t, h, :], sv[:, q, t, h, :], pb[1 + t % 2][:, e * 512 + c * P:e * 512 + (c + 1) * P])
                    last.then_inc(s["sim_red"], 1)
                v.wait_ge(s["sim_red"], 4 * i + 4)
                TH = B * RH
                svx = sv[:, 0].rearrange("p t h k -> p (t h) k").unsqueeze(3).broadcast_to([P, TH, TOPK, TOPK])
                svy = sv[:, 1].rearrange("p t h k -> p (t h) k").unsqueeze(2).broadcast_to([P, TH, TOPK, TOPK])
                lk(V.tensor_tensor(allsc[:, :, :, :], svx, svy, ALU.add))
                lk(V.tensor_copy(ivf[:, :, :, :].rearrange("p q t k -> p (q t k)"), iv[:, :, :, :, :].rearrange("p q t h k -> p (q t h k)")))
                for m in range(TH):
                    V.max(scs[:, m, :], allsc[:, m].rearrange("p a c -> p (a c)")).then_inc(s["dve"], 1)
                n[0] += TH
                v.wait_ge(s["dve"], n[0])
                for m in range(TH):
                    V.max_index(pos[:, m, :], scs[:, m, :], allsc[:, m].rearrange("p a c -> p (a c)")).then_inc(s["dve"], 1)
                n[0] += TH
                v.wait_ge(s["dve"], n[0])
                V.tensor_tensor(wsub[:, :, :], scs[:, :, :], scs[:, :, 0:1].broadcast_to([P, TH, TOPK]), ALU.subtract).then_inc(s["sub_ready"], 1)
                pf = pos[:, :, :].rearrange("p m k -> p (m k)")
                lk(V.tensor_scalar(pab[:, 0, :], pf, 3, None, ALU.logical_shift_right))
                lk(V.tensor_scalar(pab[:, 1, :], pf, 7, None, ALU.bitwise_and))
                lk(V.tensor_copy(pabf[:, :, :], pab[:, :, :]))
                for q in range(2):
                    lk(V.tensor_tensor(oh[:, :, :], pabf[:, q, :].unsqueeze(2).broadcast_to([P, TH * TOPK, TOPK]),
                                       cst[:, C_IOTA:C_IOTA + TOPK].unsqueeze(1).broadcast_to([P, TH * TOPK, TOPK]), ALU.is_equal))
                    o4 = oh[:, :, :].rearrange("p (m k) a -> p m k a", k=TOPK)
                    lk(V.tensor_tensor(o4, o4, ivf[:, q].unsqueeze(2).broadcast_to([P, TH, TOPK, TOPK]), ALU.mult))
                    lk(V.reduce_sum(isel[:, q, :], oh[:, :, :], AX.X))
                lk(V.scalar_tensor_tensor(ef[:, :], isel[:, 0, :], float(NKEY), isel[:, 1, :], ALU.mult, ALU.add))
                lk(V.tensor_scalar(ef[:, :], ef[:, :], float(NEXP - 1), None, ALU.min))
                V.tensor_copy(ei[:, :], ef[:, :]).then_inc(s["idx_ready"], 1)
                v.wait_ge(s["ex_ready"], i + 1)
                lk(V.reduce_sum(wsum[:, :], wex[:, :, :], AX.X))
                lk(V.reciprocal(wrs[:, :], wsum[:, :]))
                lk(V.tensor_tensor(wex[:, :, :], wex[:, :, :], wrs[:, :].unsqueeze(2).broadcast_to([P, TH, TOPK]), ALU.mult))
                wf = wex[:, :, :].rearrange("p (t h) k -> p t (h k)", t=B)
                lk(V.scalar_tensor_tensor(coef[:, :, 0:SLOTS - 1], ef[:, :].rearrange("p (t m) -> p t m", t=B), NEXP - 1.5, wf, ALU.is_lt, ALU.mult))
                lk(V.tensor_tensor(wf, wf, coef[:, :, 0:SLOTS - 1], ALU.subtract))
                lk(V.reduce_sum(coef[:, :, SLOTS - 1:SLOTS], wf, AX.X))
                for t in range(B):
                    v.wait_ge(s["gathered"], 16 * 32 * (4 * i + t + 1))
                    lk(V.tensor_tensor(pr[:, :, :], gbuf[:, :, 0:D], h2[:, t:t + 1, :].broadcast_to([P, SLOTS, D]), ALU.mult))
                    V.reduce_sum(wd_s[:, :], pr[:, :, :], AX.X).then_inc(s["dots"], 1)
                    v.wait_ge(s["silu_w"], 4 * i + t + 1)
                    lk(V.tensor_tensor(ws[:, :], ws[:, :], coef[:, t, :], ALU.mult))
                    lk(V.tensor_tensor(pr[:, :, :], gbuf[:, :, D:2 * D], ws[:, :].unsqueeze(2).broadcast_to([P, SLOTS, D]), ALU.mult))
                    v.sem_inc(s["g_free"], 1)
                    lk(V.reduce_sum(er[:, :], pr[:, :, :].rearrange("p k d -> p d k"), AX.X))
                    if t == 0:
                        v.wait_ge(s["mlp_ps"], i + 1)
                    lk(V.tensor_tensor(er[:, :], er[:, :], pb[3][:, t * P:(t + 1) * P], ALU.add))
                    lk(V.tensor_tensor(er[:, :], er[:, :], mod[:, t, 5, :], ALU.mult))
                    V.tensor_tensor(ot[:, :], er[:, :], x1[:, t, :], ALU.add).then_inc(s["out_ready"], 1)
                    v.wait_ge(s["out_st"], 16 * (4 * i + t + 1))


def kernel(**inputs):
    import numpy as np
    import concourse.bacc as _bacc
    from concourse.bass_utils import run_bass_kernel_spmd as _run

    nc = _bacc.Bacc("TRN2", target_bir_lowering=False, num_devices=1)
    names = ["L0_attn_hidden_states", "L0_attn_Wqkv", "L0_attn_bqkv", "L0_attn_Wd", "L0_attn_bd", "L0_ffn_Wq", "L0_ffn_keys",
             "L0_ffn_down_embed", "L0_ffn_up_embed", "L0_ffn_Wg", "L0_ffn_Wu", "L0_ffn_Wd", "L0_c", "L0_wmod"]
    arrays = {n: np.ascontiguousarray(inputs[n]) for n in names}
    arrays["constants"] = constants()
    args = [nc.dram_tensor(n, a.shape, mybir.dt.from_np(a.dtype), kind="ExternalInput").ap() for n, a in arrays.items()]
    args.append(nc.dram_tensor("out", (B, S, D), F32, kind="ExternalOutput").ap())
    adaln_block(nc, *args)
    r = _run(nc, [arrays], core_ids=[0])
    return r.results[0]["out"]
```

```python
import concourse.bass as bass
from concourse import mybir
from contextlib import ExitStack

F32 = mybir.dt.float32
BF16 = mybir.dt.bfloat16
U32 = mybir.dt.uint32
ALU = mybir.AluOpType
ACT = mybir.ActivationFunctionType
AX = mybir.AxisListType

B, S, D = 4, 1024, 128
P = 128
NI = S // P
H, HD = 16, 8
G2 = H // 2
SCALE = HD ** -0.5
EPS = 1e-5
INTER, RH, NKEY, NEXP, TOPK = 512, 4, 128, 2048, 8
HALF = 64
NB = 32
NC = P // NB
KR = 48
SLOTS = RH * TOPK + 1
BIG = -1.0e30

C_ID, C_MASK, C_BONES = 0, P, 2 * P
C_COS = C_BONES + H
C_SIN = C_COS + S
C_EYE = C_SIN + S
C_DZ = C_EYE + NB * NB
C_IOTA = C_DZ + HD + 1
C_ALL = C_IOTA + TOPK


def constants():
    import numpy as np
    c = np.zeros((P, C_ALL), np.float32)
    c[:, C_ID:C_ID + P] = np.eye(P)
    c[:, C_MASK:C_MASK + P] = np.triu(np.full((P, P), BIG), 1)
    row = np.arange(P)
    hh, d, g2 = row // 64, row // 8 % 8, row % 8
    c[row, C_BONES + 2 * g2 + hh] = 1.0
    t = np.arange(S, dtype=np.float32)
    cos, sin = np.cos(t), np.sin(t)
    c[:, C_COS:C_COS + S] = np.where(d[:, None] < 2, cos[None], 1.0)
    c[:, C_SIN:C_SIN + S] = np.where(d[:, None] == 0, -sin[None], np.where(d[:, None] == 1, sin[None], 0.0))
    c[:, C_EYE:C_EYE + NB * NB] = np.eye(NB).reshape(1, -1)
    c[:, C_DZ + HD] = 1.0
    c[:, C_IOTA:C_IOTA + TOPK] = np.arange(TOPK)
    return c


def adaln_block(nc, x, wqkv, bqkv, wd, bd, wq, keys, down, up, wg, wu, wd2, cc, wmod, cst_in, out, STOP=3, dbg=None):
    ctx = ExitStack()
    with ctx:
        def sb(name, shape, dt=F32, at=ctx):
            return at.enter_context(nc.sbuf_tensor(name, shape, dt))

        def sem(name):
            return ctx.enter_context(nc.semaphore(name))

        def dram(name, shape, dt):
            return nc.dram_tensor(name, shape, dt, kind="Internal").ap()

        qs_d = dram("qs_d", [B, 2, KR, G2, S], BF16)
        ks_d = dram("ks_d", [B, 2, KR, G2, S], BF16)
        ed_d = dram("ed_d", [B, P, G2, 2, P], F32)
        rd_d = dram("rd_d", [B * H, P], F32)
        z_d = dram("z_d", [P, 2, NB, NB], F32)
        table = dram("table", [NEXP, 2 * D], F32)

        cst = sb("cst", [P, C_ALL])
        xs = sb("xs", [P, B, NI, D])
        mod = sb("mod", [P, B, 6, D])
        wT = sb("wT", [P, 24, D])
        bdrow = sb("bdrow", [1, D])
        ones1 = sb("ones1", [1, P])
        a_all = sb("a_all", [P, B, NI, H, HD + 1])
        ident = cst[:, C_ID:C_ID + P]

        pb = [ctx.enter_context(nc.psum_tensor(f"pb{i}", [P, 1024], F32)) for i in range(4)]

        names = ("w_in", "tab_in", "c_ready", "wt_ps", "wt_sb", "silu_c", "scb", "mod_ps", "mod_sb", "setup_dve", "pool_c",
                 "bias_ps",
                 "h_ready", "hT_ps", "hT_sb", "var_ready", "sd_ready", "proj", "rope", "parts", "parts_st", "prod_ready",
                 "ld_ps", "ld_sb", "v_ps", "v_sb",
                 "m_ld", "kd_ld", "ke_ld", "ke2_ld", "q_ld", "rT_sb", "rn_ps", "max_lg", "max_red", "mx_ready", "mT_done", "qm_ready", "e_lg", "exp_done",
                 "av_done", "ed_masked", "ast_ready", "ast2_ready", "r_done", "r_evac", "ed_st", "a_ready",
                 "rd_ready", "rdT_ps", "rdT_sb", "rd_st", "x_ld", "r_ld", "es_ready", "z_ready", "z_st",
                 "vt_ld", "rr_ready", "px_done", "acur", "acc_done",
                 "ac_ready", "at_ps", "at_sb", "y_ps", "h2_ready", "var2", "sd2", "h2T_ps", "h2T_sb", "gu_ps", "sg", "act",
                 "mlp_ps", "q_ps", "q_sb", "sim_ps", "sim_red", "sub_ready", "ex_ready", "idx_ready", "gathered",
                 "dots", "silu_w", "g_free", "out_ready", "out_st", "act_own", "dve", "pool_own", "passed_dve", "passed_pe", "passed_pool")
        s = {n: sem(n) for n in names}

        def link(eng, ins, own, count):
            count[0] += 1
            ins.then_inc(own, 1)
            eng.wait_ge(own, count[0])

        def wait_alone(eng, what, value, passed):
            eng.wait_ge(s[what], value)
            eng.sem_inc(s[passed], 1)

        att = ExitStack()
        v_all = sb("v_all", [P, B, NI, H, HD], at=att)
        ldg = sb("ldg", [P, B, NI, H], at=att)
        km = sb("km", [P, G2, S], BF16, at=att)
        ke = sb("ke", [P, G2, S], BF16, at=att)
        kd = sb("kd", [P, G2, P], BF16, at=att)
        qa = sb("qa", [P, G2, P], BF16, at=att)
        mx = sb("mx", [P, G2, P], BF16, at=att)
        identb = sb("identb", [P, P], BF16, at=att)
        maskb = sb("maskb", [P, P], BF16, at=att)
        prep = ExitStack()
        wnat = sb("wnat", [P, 24, D], at=prep)
        wrow = sb("wrow", [1, 3 * D], at=prep)
        brow = sb("brow", [1, 4, P], at=prep)
        wp = sb("wp", [P, 4, P], at=prep)
        bcol = sb("bcol", [P, 4], at=prep)
        cT = sb("cT", [P, B], at=prep)
        sc = sb("sc", [P, B], at=prep)
        scb = sb("scb", [P, B, P], at=prep)
        wm = sb("wm", [P, 6 * D], at=prep)
        tmpm = sb("tmpm", [P, B, D], at=prep)
        st = sb("st", [P, NI, 6], at=prep)
        mv = sb("mv", [P, NI, 2], at=prep)
        sd = sb("sd", [P, NI], at=prep)
        rs = sb("rs", [P, NI], at=prep)
        hn = sb("hn", [P, NI, D], at=prep)
        hT = sb("hT", [P, S], at=prep)
        t1 = sb("t1", [P, S], at=prep)
        t2 = sb("t2", [P, S], at=prep)
        qf = sb("qf", [P, S], at=prep)
        kf = sb("kf", [P, S], at=prep)
        prod = sb("prod", [P, S], at=prep)
        qkp = sb("qkp", [P, 2, 3, S], BF16, at=prep)

        prep.close()
        qm = sb("qm", [P, G2, P], BF16, at=att)
        mraw = sb("mraw", [P, H, 2], at=att)
        mfin = sb("mfin", [P, H], at=att)
        esub = sb("esub", [P, B, H], at=att)
        es = sb("es", [P, B, H], at=att)
        et = sb("et", [P, 2, 8, P], at=att)
        ed = sb("ed", [P, G2, 2, P], at=att)
        ast = sb("ast", [P, NI - 1, H, HD + 1], at=att)
        rsb = sb("rsb", [P, B, H, HD + 1], at=att)
        rdn = sb("rdn", [P, B, H], at=att)
        rn = sb("rn", [P, B, H, HD], at=att)
        rdT = sb("rdT", [B * H, P], at=att)
        xb = sb("xb", [P, 2, NB, NB], at=att)
        rdb = sb("rdb", [P, 2, NB], at=att)
        zb = sb("zb", [P, 2, NB, NB], at=att)
        tb = sb("tb", [P, 2, NB, NB], at=att)
        edb = sb("edb", [P, 2, H, P], at=att)
        vtb = sb("vtb", [P, 2, H, NB], at=att)
        rts = sb("rts", [P, 4, P], at=att)
        rr = sb("rr", [P, 2, H, HD], at=att)
        acur = sb("acur", [P, 2, H, HD], at=att)
        att.close()

        ffn = ctx
        gbuf = sb("gbuf", [P, SLOTS, 2 * D], at=ffn)
        pr = sb("pr", [P, SLOTS, D], at=ffn)
        ac = sb("ac", [P, B, H, HD], at=ffn)
        aT = sb("aT", [P, B, P], at=ffn)
        x1 = sb("x1", [P, B, D], at=ffn)
        tf = sb("tf", [P, B, D], at=ffn)
        h2 = sb("h2", [P, B, D], at=ffn)
        h2T = sb("h2T", [P, B, P], at=ffn)
        st2 = sb("st2", [P, B, 6], at=ffn)
        mv2 = sb("mv2", [P, B, 2], at=ffn)
        sd2 = sb("sd2t", [P, B], at=ffn)
        rs2 = sb("rs2", [P, B], at=ffn)
        sg = sb("sgt", [P, 2, 512], at=ffn)
        hid = sb("hid", [P, 4, B, P], at=ffn)
        qT = sb("qT", [P, 4, B, P], at=ffn)
        sv = sb("sv", [P, 2, B, RH, TOPK], at=ffn)
        iv = sb("iv", [P, 2, B, RH, TOPK], U32, at=ffn)
        ivf = sb("ivf", [P, 2, B * RH, TOPK], at=ffn)
        allsc = sb("allsc", [P, B * RH, TOPK, TOPK], at=ffn)
        scs = sb("scs", [P, B * RH, TOPK], at=ffn)
        pos = sb("pos", [P, B * RH, TOPK], U32, at=ffn)
        pab = sb("pab", [P, 2, B * RH * TOPK], U32, at=ffn)
        pabf = sb("pabf", [P, 2, B * RH * TOPK], at=ffn)
        oh = sb("oh", [P, B * RH * TOPK, TOPK], at=ffn)
        isel = sb("isel", [P, 2, B * RH * TOPK], at=ffn)
        ef = sb("ef", [P, B * RH * TOPK], at=ffn)
        ei = sb("ei", [P, B * RH * TOPK], U32, at=ffn)
        wsub = sb("wsub", [P, B * RH, TOPK], at=ffn)
        wex = sb("wex", [P, B * RH, TOPK], at=ffn)
        wsum = sb("wsum", [P, B * RH], at=ffn)
        wrs = sb("wrs", [P, B * RH], at=ffn)
        coef = sb("coef", [P, B, SLOTS], at=ffn)
        wd_s = sb("wd_s", [P, SLOTS], at=ffn)
        ws = sb("ws", [P, SLOTS], at=ffn)
        er = sb("er", [P, D], at=ffn)
        ot = sb("ot", [P, D], at=ffn)
        print("sbuf left", nc.sbuf_bytes_remaining)

        def chunks_before(i):
            return 4 * sum(2 * (j + 1) for j in range(i))

        def chunk(i, b, n):
            return chunks_before(i) + b * (2 * (i + 1)) + n

        def mcount(i):
            return H * (1 if i < 4 else 2)

        def mlg(i, b, n):
            return 4 * sum(mcount(j) for j in range(i)) + b * mcount(i) + n

        def off(i, b, n):
            return 4 * sum(2 * j for j in range(i)) + b * (2 * i) + n

        def blocks(i, n):
            res = []
            for k in range(4):
                for hh in range(2):
                    g2, j = (4 * n + k, i) if n < 2 else (4 * (n % 2) + k, (n - 2) // 2)
                    res.append((hh * 4 + k, g2, hh, j))
            return res

        rT = pb[3][:, 0:512].rearrange("p (g n) -> p g n", g=4)
        rback = pb[3][:, 512:1024].rearrange("p (g q d) -> p g q d", g=4, q=4)
        px = [t.rearrange("p (h d) -> p h d", h=H) for t in (pb[3][:, 512:640], pb[1][:, 0:128])]
        pacc = [t.rearrange("p (h d) -> p h d", h=H) for t in (pb[1][:, 512:640], pb[2][:, 0:128])]

        block = ctx.enter_context(nc.Block())
        NSETUP_IN = [0]

        @block.sync
        def _(sp):
            w = s["w_in"]

            def ld(dst, src):
                sp.dma_start(dst, src).then_inc(w, 16)
                NSETUP_IN[0] += 1
            ld(cst[:, :], cst_in)
            ld(wnat[:, 0:3, :], wqkv.rearrange("(t p) d -> p t d", p=P))
            ld(wnat[:, 3, :], wd)
            ld(wnat[:, 4:8, :], wq.rearrange("(t p) d -> p t d", p=P))
            ld(wnat[:, 8:12, :], wg.rearrange("(t p) d -> p t d", p=P))
            ld(wnat[:, 12:16, :], wu.rearrange("(t p) d -> p t d", p=P))
            ld(wnat[:, 16:20, :], wd2.rearrange("p (t d) -> p t d", d=P))
            kn = wnat[:, 20:24, :].rearrange("k (q m) (e n) -> k q m e n", q=2, e=2)
            for h in range(RH):
                ld(kn[:, :, h // 2, h % 2, :], keys[h])
            ld(wrow[:, :], bqkv.rearrange("(a n) -> a n", a=1))
            ld(bdrow[:, :], bd.rearrange("(a n) -> a n", a=1))
            with nc.allow_non_contiguous_dma(reason="512 elements"):
                ld(cT[:, :], cc.rearrange("b k -> k b"))
            ld(wm[:, :], wmod)
            for b in range(B):
                ld(xs[:, b, :, :], x[b].rearrange("(i p) d -> p i d", p=P))
            sp.dma_start(table[:, 0:D], down).then_inc(s["tab_in"], 16)
            sp.dma_start(table[:, D:2 * D], up).then_inc(s["tab_in"], 16)
            with sp.Fori(0, B) as b:
                for qk, dst, order in ((0, qs_d, (0, 0, 1, 1, 0, 2)), (1, ks_d, (0, 1, 0, 1, 2, 0))):
                    sp.wait_ge(s["parts"], 2 * b + qk + 1)
                    for hh in range(2):
                        for r, part in enumerate(order):
                            sp.dma_start(dst[b, hh, r * HD:(r + 1) * HD, :, :].rearrange("d g s -> (d g) s"),
                                         qkp[64 * hh:64 * hh + 64, qk, part, :]).then_inc(s["parts_st"], 16)
            sp.wait_ge(s["parts_st"], 16 * 24 * B)
            if STOP < 2:
                return
            sp.wait_ge(s["pool_c"], 1)
            sp.sem_inc(s["ed_st"], 16)
            steps = [(i, b) for i in range(NI) for b in range(B)]

            def load_km(i, b):
                for hh in range(2):
                    sp.dma_start(km[64 * hh:64 * hh + KR, :, 0:(i + 1) * P], ks_d[b, hh, :, :, 0:(i + 1) * P]).then_inc(s["m_ld"], 16)

            def load_qa(i, b):
                for hh in range(2):
                    sp.dma_start(qa[64 * hh:64 * hh + KR, :, :], qs_d[b, hh, :, :, i * P:(i + 1) * P]).then_inc(s["q_ld"], 16)

            def load_kd(i, b):
                for hh in range(2):
                    sp.dma_start(kd[64 * hh:64 * hh + KR, :, :], ks_d[b, hh, :, :, i * P:(i + 1) * P]).then_inc(s["kd_ld"], 16)

            def load_ke(i, b, part):
                half = (i + 1) // 2
                j0, j1 = ((0, half), (half, i))[part]
                for hh in range(2):
                    sp.dma_start(ke[64 * hh:64 * hh + KR, :, j0 * P:j1 * P], ks_d[b, hh, :, :, j0 * P:j1 * P]
                                 ).then_inc(s[("ke_ld", "ke2_ld")[part]], 16)
            load_km(0, 0)
            load_qa(0, 0)
            load_kd(0, 0)
            sp.wait_ge(s["mx_ready"], 1)
            load_km(0, 1)
            for n, (i, b) in enumerate(steps):
                after = steps[n + 1] if n + 1 < len(steps) else None
                half = (i + 1) // 2
                if after:
                    ia, ha = after[0], (after[0] + 1) // 2
                    sp.wait_ge(s["qm_ready"], n + 1)
                    load_qa(*after)
                    sp.wait_ge(s["e_lg"], chunk(i, b, 1) + 1)
                    load_kd(*after)
                sp.wait_ge(s["ed_masked"], n + 1)
                sp.dma_start(ed_d[b], ed[:, :, :, :]).then_inc(s["ed_st"], 16)
                sp.wait_ge(s["ed_st"], 16 * (n + 2))
                for c in range(NC):
                    sp.dma_start(xb[b * 32 + c * 8:b * 32 + c * 8 + 8, :, :, :],
                                 ed_d[b, c * NB:(c + 1) * NB, :, :, c * NB:(c + 1) * NB].rearrange("j g e i -> g e j i")
                                 ).then_inc(s["x_ld"], 16)
                if after:
                    if ia:
                        sp.wait_ge(s["e_lg"], chunk(i, b, 2 + 2 * min(ha, i) - 1) + 1)
                        load_ke(*after, 0)
                    if n + 2 < len(steps):
                        sp.wait_ge(s["mx_ready"], n + 2)
                        load_km(*steps[n + 2])
                    if ia > ha:
                        sp.wait_ge(s["e_lg"], chunk(i, b, 2 * (i + 1) - 1) + 1)
                        load_ke(*after, 1)
                if b == B - 1:
                    sp.wait_ge(s["rdT_sb"], i + 1)
                    sp.dma_start(rd_d, rdT[:, :]).then_inc(s["rd_st"], 16)
                    sp.wait_ge(s["rd_st"], 16 * (i + 1))
                    rv = rd_d.rearrange("(b g e) (c n) -> b c g e n", b=B, e=2, c=NC)
                    for bb in range(B):
                        for c in range(NC):
                            sp.dma_start(rdb[bb * 32 + c * 8:bb * 32 + c * 8 + 8, :, :], rv[bb, c]).then_inc(s["r_ld"], 16)
                    sp.wait_ge(s["z_ready"], i + 1)
                    sp.dma_start(z_d, zb[:, :, :, :]).then_inc(s["z_st"], 16)
                    sp.wait_ge(s["z_st"], 16 * (i + 1))
                    zv = z_d.rearrange("(b c g) e k i -> b c k (g e) i", b=B, c=NC)
                    for pair in range(B // 2):
                        sp.wait_ge(s["a_ready"], 4 * i + 2 * pair + 1)
                        for m in range(2):
                            sp.dma_start(edb[:, m, :, :], ed_d[2 * pair + m].rearrange("j g e i -> j (g e) i")).then_inc(s["vt_ld"], 16)
                            for c in range(NC):
                                sp.dma_start(vtb[c * NB:(c + 1) * NB, m, :, :], zv[2 * pair + m, c]).then_inc(s["vt_ld"], 16)
            if STOP < 3:
                return
            sp.wait_ge(s["tab_in"], 32)
            sp.wait_ge(s["pool_c"], 2)
            sp.dma_start(gbuf[:, SLOTS - 1, :], table[NEXP - 1:NEXP, :].broadcast_to([P, 2 * D])).then_inc(s["tab_in"], 16)
            with sp.Fori(0, NI) as i:
                for t in range(B):
                    sp.wait_ge(s["out_ready"], 4 * i + t + 1)
                    sp.dma_start(out[t, bass.ds(i * P, P), :], ot[:, :]).then_inc(s["out_st"], 16)
            sp.wait_ge(s["out_st"], 16 * B * NI)

        @block.gpsimd
        def _(g):
            nc.gpsimd.memset(ones1[:, :], 1.0).then_inc(s["c_ready"], 1)
            nc.gpsimd.memset(km[:, :, :], 1.0).then_inc(s["c_ready"], 1)
            nc.gpsimd.memset(ke[:, :, :], 1.0).then_inc(s["c_ready"], 1)
            nc.gpsimd.memset(kd[:, :, :], 1.0).then_inc(s["c_ready"], 1)
            nc.gpsimd.memset(qa[:, :, :], 0.0).then_inc(s["c_ready"], 1)
            nc.gpsimd.memset(mx[:, :, :], 0.0).then_inc(s["c_ready"], 1)
            nc.gpsimd.memset(a_all[:, :, :, :, :], 1.0).then_inc(s["c_ready"], 1)
            g.wait_ge(s["c_ready"], 7)
            g.sem_inc(s["pool_c"], 1)
            zero = g.to_reg(0.0)
            last_gathered = g.to_reg(NEXP - 2)
            if STOP < 2:
                return
            for i in range(NI):
                half = (i + 1) // 2
                with g.Fori(0, B) as b:
                    step = 4 * i + b
                    if i:
                        g.wait_ge(s["a_ready"], 4 * i + 1)
                        g.wait_ge(s["av_done"], off(i, b, 0) - 2 * (i - half) + 2)
                        nc.gpsimd.tensor_copy(ast[:, 0:half, :, :], a_all[:, b, 0:half, :, :]).then_inc(s["ast_ready"], 1)
                        if i > half:
                            wait_alone(g, "r_done", step, "passed_pool")
                            nc.gpsimd.tensor_copy(ast[:, half:i, :, :], a_all[:, b, half:i, :, :]).then_inc(s["ast2_ready"], 1)
                    wait_alone(g, "exp_done", chunk(i, b, 1) + 1 + 2, "passed_pool")
                    nc.gpsimd.affine_select(out=ed[:, :, :, :], in_=ed[:, :, :, :], compare_op=ALU.is_ge, fill=zero, base=0,
                                            pattern=[[0, 2], [0, G2], [1, P]], channel_multiplier=-1).then_inc(s["ed_masked"], 1)
            if STOP < 3:
                return
            g.wait_ge(s["a_ready"], 4 * NI + 1)
            nc.gpsimd.memset(gbuf[:, :, :], 0.0).then_inc(s["pool_own"], 1)
            g.wait_ge(s["pool_own"], 1)
            g.sem_inc(s["pool_c"], 1)
            g.wait_ge(s["tab_in"], 48)
            with g.Fori(0, NI) as i:
                g.wait_ge(s["at_ps"], i + 1)
                nc.gpsimd.tensor_copy(ac[:, :, :, :], a_all[:, :, i, :, 0:HD]).then_inc(s["ac_ready"], 1)
                wait_alone(g, "idx_ready", i + 1, "passed_pool")
                for t in range(B):
                    wait_alone(g, "g_free", 4 * i + t + 1, "passed_pool")
                    for k in range(SLOTS - 1):
                        nc.gpsimd.indirect_dma_start(gbuf[:, k, :], None, table,
                                                     bass.IndirectOffsetOnAxis(ei[:, t * 32 + k:t * 32 + k + 1], 0),
                                                     bounds_check=last_gathered, oob_is_err=False).then_inc(s["gathered"], 16)

        @block.scalar
        def _(a):
            a.wait_ge(s["w_in"], 16 * NSETUP_IN[0])
            nc.scalar.activation(sc[:, :], cT[:, :], ACT.Silu).then_inc(s["silu_c"], 1)
            for n in range(6):
                a.wait_ge(s["wt_ps"], n + 1)
                nc.scalar.activation(wT[:, 4 * n:4 * n + 4, :], pb[n % 4][:, 0:512].rearrange("p (t d) -> p t d", d=D), ACT.Copy).then_inc(s["wt_sb"], 1)
            with a.Fori(0, B) as b:
                a.wait_ge(s["var_ready"], b + 1)
                nc.scalar.activation(sd[:, :], rs[:, :], ACT.Sqrt).then_inc(s["sd_ready"], 1)
                a.wait_ge(s["hT_ps"], b + 1)
                nc.scalar.activation(hT[:, :], pb[0][:, :], ACT.Copy).then_inc(s["hT_sb"], 1)
                a.wait_ge(s["v_ps"], b + 1)
                nc.scalar.activation(v_all[:, b, :, :, :].rearrange("p i h d -> p (i h d)"), pb[0][:, :], ACT.Copy).then_inc(s["v_sb"], 1)
                a.wait_ge(s["ld_ps"], b + 1)
                nc.scalar.activation(ldg[:, b, :, :].rearrange("p i h -> p (i h)"), pb[3][:, 0:NI * H], ACT.Copy).then_inc(s["ld_sb"], 1)
            if STOP < 2:
                return
            a.sem_inc(s["exp_done"], 2)
            def exps(i, b):
                step = 4 * i + b
                for n in range(2 * (i + 1)):
                    a.wait_ge(s["e_lg"], chunk(i, b, n) + 1)
                    src = pb[1 + n % 2][:, :].rearrange("p (e k i) -> p e k i", e=2, k=4)
                    if n < 2:
                        if n == 0:
                            a.wait_ge(s["ed_st"], 16 * (step + 1))
                        dst = ed[:, 4 * n:4 * n + 4, :, :].rearrange("p k e i -> p e k i")
                    else:
                        a.wait_ge(s["av_done"], off(i, b, n - 2) + 1)
                        dst = et[:, n % 2, :, :].rearrange("p (e k) i -> p e k i", e=2)
                    nc.scalar.activation(dst, src, ACT.Exp, scale=SCALE).then_inc(s["exp_done"], 1)
                a.wait_ge(s["r_done"], step + 1)
                nc.scalar.activation(rts[:, :, :].rearrange("p g n -> p (g n)"), pb[3][:, 0:512], ACT.Copy).then_inc(s["rT_sb"], 1)
            for i in range(NI):
                with a.Fori(0, B - 1) as b:
                    exps(i, b)
                a.wait_ge(s["mx_ready"], 4 * (i + 1))
                nc.scalar.activation(es[:, :, :], esub[:, :, :], ACT.Exp, scale=SCALE).then_inc(s["es_ready"], 1)
                exps(i, B - 1)
                with a.Fori(0, B // 2) as pair:
                    for c in range(NC):
                        rows = slice(c * NB, (c + 1) * NB)
                        for m in range(2):
                            n = 8 * (2 * i + pair) + 2 * c + m
                            a.wait_ge(s["px_done"], n + 1)
                            if c == 0:
                                a.wait_ge(s["a_ready"], 4 * i + 2 * pair + 1)
                            nc.scalar.activation(acur[rows, m, :, :], px[m][rows, :, :], ACT.Copy).then_inc(s["acur"], 1)
            if STOP < 3:
                return
            with a.Fori(0, NI) as i:
                a.wait_ge(s["at_ps"], i + 2)
                nc.scalar.activation(aT[:, :, :].rearrange("p b n -> p (b n)"), pb[0][:, 0:512], ACT.Copy).then_inc(s["at_sb"], 1)
                a.wait_ge(s["var2"], i + 1)
                nc.scalar.activation(sd2[:, :], rs2[:, :], ACT.Sqrt).then_inc(s["sd2"], 1)
                a.wait_ge(s["h2T_ps"], i + 1)
                nc.scalar.activation(h2T[:, :, :].rearrange("p b n -> p (b n)"), pb[0][:, 0:512], ACT.Copy).then_inc(s["h2T_sb"], 1)
                for c in range(4):
                    a.wait_ge(s["gu_ps"], 4 * i + c + 1)
                    if c >= 2:
                        a.wait_ge(s["act"], 4 * i + c - 1)
                    nc.scalar.activation(sg[:, c % 2, :], pb[1 + c % 2][:, 0:512], ACT.Silu).then_inc(s["sg"], 1)
                for c in range(4):
                    a.wait_ge(s["q_ps"], 4 * i + c + 1)
                    nc.scalar.activation(qT[:, c, :, :].rearrange("p b n -> p (b n)"), pb[0][:, (c % 2) * 512:(c % 2) * 512 + 512], ACT.Copy).then_inc(s["q_sb"], 1)
                a.wait_ge(s["sub_ready"], i + 1)
                nc.scalar.activation(wex[:, :, :], wsub[:, :, :], ACT.Exp).then_inc(s["ex_ready"], 1)
                for t in range(B):
                    a.wait_ge(s["dots"], 4 * i + t + 1)
                    nc.scalar.activation(ws[:, :], wd_s[:, :], ACT.Silu).then_inc(s["silu_w"], 1)

        @block.tensor
        def _(pe):
            mm = nc.tensor.matmul
            pe.wait_ge(s["w_in"], 16 * NSETUP_IN[0])
            for n in range(6):
                if n >= 4:
                    pe.wait_ge(s["wt_sb"], n - 3)
                for t in range(4):
                    last = mm(pb[n % 4][:, t * P:(t + 1) * P], wnat[:, 4 * n + t, :], ident, start=True, stop=True)
                last.then_inc(s["wt_ps"], 1)
            pe.wait_ge(s["scb"], 1)
            pe.wait_ge(s["wt_sb"], 6)
            for b in range(B):
                if b:
                    pe.wait_ge(s["mod_sb"], b)
                mm(pb[0][:, 0:512], scb[:, b, :], wm[:, 0:512], start=True, stop=True)
                mm(pb[0][:, 512:768], scb[:, b, :], wm[:, 512:768], start=True, stop=True).then_inc(s["mod_ps"], 1)
            pe.wait_ge(s["c_ready"], 7)
            pe.wait_ge(s["setup_dve"], 1)
            for n in range(4):
                last = mm(pb[3][:, n:n + 1], brow[0:1, n, :], ones1[0:1, 0:1], start=True, stop=True)
            last.then_inc(s["bias_ps"], 1)
            with pe.Fori(0, B) as b:
                pe.wait_ge(s["h_ready"], b + 1)
                for t in range(NI):
                    last = mm(pb[0][:, t * P:(t + 1) * P], hn[:, t, :], ident, start=True, stop=True)
                last.then_inc(s["hT_ps"], 1)
                pe.wait_ge(s["hT_sb"], b + 1)
                for t in range(NI):
                    mm(pb[0][:, t * P:(t + 1) * P], hT[:, t * P:(t + 1) * P], wT[:, 2, :], start=True, stop=False)
                    last = mm(pb[0][:, t * P:(t + 1) * P], ones1[0:1, :], wrow[0:1, 2 * D:3 * D], start=False, stop=True)
                last.then_inc(s["v_ps"], 1)
                for qk in range(2):
                    if qk:
                        pe.wait_ge(s["rope"], 2 * b + 1)
                    for w in range(2):
                        for half in range(2):
                            last = mm(pb[1 + w][:, half * 512:(half + 1) * 512], wp[:, 2 * qk + w, :], hT[:, half * 512:(half + 1) * 512], start=True, stop=True)
                    last.then_inc(s["proj"], 1)
                pe.wait_ge(s["prod_ready"], b + 1)
                for t in range(NI):
                    last = mm(pb[3][:, t * H:(t + 1) * H], prod[:, t * P:(t + 1) * P], cst[:, C_BONES:C_BONES + H], start=True, stop=True)
                last.then_inc(s["ld_ps"], 1)
                pe.wait_ge(s["v_sb"], b + 1)
                pe.wait_ge(s["ld_sb"], b + 1)
            pe.sem_inc(s["av_done"], 2)
            if STOP < 2:
                return

            def max_units(i, b):
                n = 0
                for h in range(H):
                    g2, hh = h // 2, h % 2
                    for c0 in range(0, (i + 1) * P, 512):
                        c1 = min(c0 + 512, (i + 1) * P)
                        if n == 0:
                            pe.wait_ge(s["m_ld"], 32 * (4 * i + b + 1))
                            pe.wait_ge(s["q_ld"], 32 * (4 * i + b + 1))
                        bank = pb[0][:, (n % 2) * 512:(n % 2) * 512 + 512]
                        if n >= 2:
                            pe.wait_ge(s["max_red"], mlg(i, b, n - 1))
                        last = mm(bank[:, 0:c1 - c0], qa[64 * hh:64 * hh + KR, g2, :], km[64 * hh:64 * hh + KR, g2, c0:c1],
                                  start=True, stop=c1 < (i + 1) * P)
                        if c1 == (i + 1) * P:
                            last = mm(bank[:, i * P - c0:i * P - c0 + P], identb[:, :], maskb[:, :], start=False, stop=True)
                        last.then_inc(s["max_lg"], 1)
                        n += 1
                        yield

            def turn_maxima(i, b):
                pe.wait_ge(s["mx_ready"], 4 * i + b + 1)
                for g2 in range(G2):
                    last = mm(pb[0][:, g2 * P:(g2 + 1) * P], mx[:, g2, :], identb[:, :], start=True, stop=True)
                last.then_inc(s["mT_done"], 1)

            def attend(i, b, after):
                step = 4 * i + b
                total = 2 * (i + 1)
                half = (i + 1) // 2
                units = max_units(*after) if after else iter(())
                share = -(-mcount(after[0]) // total) if after else 0
                started = set()

                def multiply(n):
                    if n >= 2:
                        pe.wait_ge(s["exp_done"], chunk(i, b, n) + 3)
                        if n == 2:
                            pe.wait_ge(s["ast_ready"], 4 * (i - 1) + b + 1)
                        if n == 2 + 2 * half:
                            pe.wait_ge(s["ast2_ready"], 4 * (i - 2) + b + 1)
                    elif n == 0:
                        pe.wait_ge(s["ed_masked"], step + 1)
                    for k, g2, hh, j in blocks(i, n):
                        h = 2 * g2 + hh
                        q = h % 4
                        rhs = et[:, n % 2, k, :] if n >= 2 else ed[:, g2, hh, :]
                        lhs = ast[:, j, h, :] if n >= 2 else cst[:, C_DZ:C_DZ + HD + 1]
                        last = mm(rT[32 * q:32 * q + HD + 1, h // 4, :], lhs, rhs, start=q not in started, stop=True, skip_group_check=True)
                        started.add(q)
                    return last
                pe.wait_ge(s["kd_ld"], 32 * (step + 1))
                pe.wait_ge(s["qm_ready"], step + 1)
                for n in range(total):
                    pe.wait_ge(s["exp_done"], chunk(i, b, n) + 1)
                    if n == 2:
                        pe.wait_ge(s["ke_ld"], 32 * (4 * (i - 1) + b + 1))
                    if n == 2 + 2 * half:
                        pe.wait_ge(s["ke2_ld"], 32 * (4 * (i - 2) + b + 1))
                    for k, g2, hh, j in blocks(i, n):
                        keys_of = kd[64 * hh:64 * hh + KR + 2, g2, :] if n < 2 else ke[64 * hh:64 * hh + KR + 2, g2, j * P:(j + 1) * P]
                        last = mm(pb[1 + n % 2][:, k * P:(k + 1) * P], keys_of, qm[64 * hh:64 * hh + KR + 2, g2, :], start=True, stop=True)
                    last.then_inc(s["e_lg"], 1)
                    for _ in range(share):
                        next(units, None)
                    if n >= 3:
                        multiply(n - 1).then_inc(s["av_done"], 1)
                for _ in units:
                    pass
                if total > 2:
                    multiply(total - 1).then_inc(s["av_done"], 1)
                if after:
                    turn_maxima(*after)
                multiply(0)
                multiply(1).then_inc(s["r_done"], 1)
                pe.wait_ge(s["rT_sb"], step + 1)
                if i:
                    pe.wait_ge(s["r_evac"], step)
                for g4 in range(4):
                    last = mm(pb[3][:, 512 + g4 * P:512 + (g4 + 1) * P], rts[:, g4, :], ident, start=True, stop=True)
                last.then_inc(s["rn_ps"], 1)
            for _ in max_units(0, 0):
                pass
            turn_maxima(0, 0)
            for i in range(NI):
                with pe.Fori(0, B - 1) as b:
                    attend(i, b, (i, b + 1))
                attend(i, B - 1, (i + 1, 0) if i < NI - 1 else None)
                pe.wait_ge(s["rd_ready"], i + 1)
                mm(pb[1][0:B * H, 0:P], rdn[:, :, :].rearrange("p b h -> p (b h)"), ident, start=True, stop=True).then_inc(s["rdT_ps"], 1)
                with pe.Fori(0, B // 2) as pair:
                    two = 2 * i + pair
                    pe.wait_ge(s["vt_ld"], 2 * 16 * 5 * (two + 1))
                    for c in range(NC):
                        rows = slice(c * NB, (c + 1) * NB)
                        for m in range(2):
                            wait_alone(pe, "rr_ready", 8 * two + 2 * c + m + 1, "passed_pe")
                            for h in range(H):
                                last = mm(px[m][rows, h, :], vtb[rows, m, h, :], rr[rows, m, h, :], start=True, stop=True, skip_group_check=True)
                            last.then_inc(s["px_done"], 1)
                        if c < NC - 1:
                            for m in range(2):
                                wait_alone(pe, "acur", 8 * two + 2 * c + m + 1, "passed_pe")
                                for h in range(H):
                                    for to in range(c + 1, NC):
                                        last = mm(pacc[m][to * NB:(to + 1) * NB, h, :], edb[rows, m, h, to * NB:(to + 1) * NB],
                                                  acur[rows, m, h, :], start=(c == 0 and h == 0), stop=True, skip_group_check=True)
                                last.then_inc(s["acc_done"], 1)
                pe.wait_ge(s["acur"], 16 * (i + 1))
            if STOP < 3:
                return
            pe.sem_inc(s["at_ps"], 1)
            with pe.Fori(0, NI) as i:
                pe.wait_ge(s["ac_ready"], i + 1)
                for t in range(B):
                    last = mm(pb[0][:, t * P:(t + 1) * P], ac[:, t, :, :].rearrange("p h d -> p (h d)"), ident, start=True, stop=True)
                last.then_inc(s["at_ps"], 1)
                pe.wait_ge(s["at_sb"], i + 1)
                for t in range(B):
                    mm(pb[0][:, 512 + t * P:512 + (t + 1) * P], aT[:, t, :], wT[:, 3, :], start=True, stop=False)
                    last = mm(pb[0][:, 512 + t * P:512 + (t + 1) * P], ones1[0:1, :], bdrow[0:1, :], start=False, stop=True)
                last.then_inc(s["y_ps"], 1)
                pe.wait_ge(s["h2_ready"], i + 1)
                for t in range(B):
                    last = mm(pb[0][:, t * P:(t + 1) * P], h2[:, t, :], ident, start=True, stop=True)
                last.then_inc(s["h2T_ps"], 1)
                pe.wait_ge(s["h2T_sb"], i + 1)
                hx = h2T[:, :, :].rearrange("p b n -> p (b n)")
                for c in range(4):
                    if c >= 2:
                        pe.wait_ge(s["act"], 4 * i + c - 1)
                    mm(pb[1 + c % 2][:, 0:512], wT[:, 8 + c, :], hx, start=True, stop=True)
                    mm(pb[1 + c % 2][:, 512:1024], wT[:, 12 + c, :], hx, start=True, stop=True).then_inc(s["gu_ps"], 1)
                for c in range(4):
                    if c >= 2:
                        pe.wait_ge(s["q_sb"], 4 * i + c - 1)
                    mm(pb[0][:, (c % 2) * 512:(c % 2) * 512 + 512], wT[:, 4 + c, :], hx, start=True, stop=True).then_inc(s["q_ps"], 1)
                pe.wait_ge(s["act"], 4 * i + 4)
                for t in range(B):
                    for c in range(4):
                        last = mm(pb[3][:, t * P:(t + 1) * P], hid[:, c, t, :], wT[:, 16 + c, :], start=c == 0, stop=c == 3)
                last.then_inc(s["mlp_ps"], 1)
                pe.wait_ge(s["q_sb"], 4 * i + 4)
                for t in range(B):
                    if t >= 2:
                        pe.wait_ge(s["sim_red"], 4 * i + t - 1)
                    for q in range(2):
                        for h in range(RH):
                            c, e = 2 * q + h // 2, h % 2
                            last = mm(pb[1 + t % 2][:, e * 512 + c * P:e * 512 + (c + 1) * P], qT[64 * e:64 * e + 64, c, t, :],
                                      wT[64 * e:64 * e + 64, 20 + c, :], start=True, stop=True)
                    last.then_inc(s["sim_ps"], 1)
                pe.wait_ge(s["out_ready"], 4 * i + 4)

        @block.vector
        def _(v):
            V = nc.vector
            n = [0]

            def lk(ins):
                link(v, ins, s["dve"], n)

            def restart():
                v.sem_clear(s["dve"])
                n[0] = 0
            v.wait_ge(s["w_in"], 16 * NSETUP_IN[0])
            v.wait_ge(s["c_ready"], 7)
            V.tensor_copy(identb[:, :], ident)
            lk(V.tensor_copy(maskb[:, :], cst[:, C_MASK:C_MASK + P]))
            v.wait_ge(s["wt_sb"], 1)
            for qk in range(2):
                src = wT[:, qk, :].rearrange("p (g e d) -> p e d g", g=G2, e=2)
                bsrc = wrow[0:1, qk * D:(qk + 1) * D].rearrange("p (g e d) -> p e d g", g=G2, e=2)
                for w in range(2):
                    dst = wp[:, 2 * qk + w, :].rearrange("p (e d g) -> p e d g", e=2, g=G2)
                    bdst = brow[0:1, 2 * qk + w, :].rearrange("p (e d g) -> p e d g", e=2, g=G2)
                    for dd, ss in ((dst, src), (bdst, bsrc)):
                        for e in range(2):
                            if w == 0:
                                lk(V.tensor_copy(dd[:, e], ss[:, e]))
                            else:
                                lk(V.tensor_copy(dd[:, e, 2:8], ss[:, e, 2:8]))
                                lk(V.tensor_copy(dd[:, e, 0], ss[:, e, 1]))
                                lk(V.tensor_copy(dd[:, e, 1], ss[:, e, 0]))
            v.sem_inc(s["setup_dve"], 1)
            v.wait_ge(s["silu_c"], 1)
            V.tensor_copy(scb[:, :, :], sc[:, :].unsqueeze(2).broadcast_to([P, B, P])).then_inc(s["scb"], 1)
            for b in range(B):
                v.wait_ge(s["mod_ps"], b + 1)
                V.tensor_copy(mod[:, b, :, :].rearrange("p m d -> p (m d)"), pb[0][:, 0:768]).then_inc(s["mod_sb"], 1)
            v.wait_ge(s["mod_sb"], B)
            for m in (1, 4):
                lk(V.tensor_scalar(mod[:, :, m, :], mod[:, :, m, :], 1.0, None, ALU.add))
            for m in (2, 5):
                lk(V.tensor_scalar(tmpm[:, :, :], mod[:, :, m, :], -1.0, 0.25, ALU.mult, ALU.max))
                lk(V.tensor_tensor(tmpm[:, :, :], tmpm[:, :, :], mod[:, :, m, :], ALU.max))
                lk(V.tensor_scalar(mod[:, :, m, :], mod[:, :, m, :], 0.0, 2.0, ALU.is_ge, ALU.mult))
                lk(V.tensor_scalar(mod[:, :, m, :], mod[:, :, m, :], -1.0, None, ALU.add))
                lk(V.tensor_tensor(mod[:, :, m, :], mod[:, :, m, :], tmpm[:, :, :], ALU.mult))
            v.wait_ge(s["bias_ps"], 1)
            lk(V.tensor_copy(bcol[:, :], pb[3][:, 0:4]))
            with v.Fori(0, B) as b:
                restart()
                for t in range(NI):
                    V.bn_stats(st[:, t, :], xs[:, b, t, :]).then_inc(s["dve"], 1)
                n[0] += NI
                v.wait_ge(s["dve"], n[0])
                for t in range(NI):
                    V.bn_aggr(mv[:, t, :], st[:, t, :]).then_inc(s["dve"], 1)
                n[0] += NI
                v.wait_ge(s["dve"], n[0])
                V.tensor_scalar(rs[:, :], mv[:, :, 1], EPS, None, ALU.add).then_inc(s["var_ready"], 1)
                v.wait_ge(s["sd_ready"], b + 1)
                lk(V.reciprocal(rs[:, :], sd[:, :]))
                for t in range(NI):
                    V.tensor_scalar(hn[:, t, :], xs[:, b, t, :], mv[:, t, 0:1], rs[:, t:t + 1], ALU.subtract, ALU.mult).then_inc(s["dve"], 1)
                n[0] += NI
                v.wait_ge(s["dve"], n[0])
                lk(V.tensor_tensor(hn[:, :, :], hn[:, :, :], mod[:, b, 1:2, :].broadcast_to([P, NI, D]), ALU.mult))
                V.tensor_tensor(hn[:, :, :], hn[:, :, :], mod[:, b, 0:1, :].broadcast_to([P, NI, D]), ALU.add).then_inc(s["h_ready"], 1)
                for qk, res in ((0, qf), (1, kf)):
                    v.wait_ge(s["proj"], 2 * b + qk + 1)
                    V.scalar_tensor_tensor(t1[:, :], pb[1][:, :], bcol[:, 2 * qk:2 * qk + 1], cst[:, C_COS:C_COS + S], ALU.add, ALU.mult).then_inc(s["dve"], 1)
                    V.scalar_tensor_tensor(t2[:, :], pb[2][:, :], bcol[:, 2 * qk + 1:2 * qk + 2], cst[:, C_SIN:C_SIN + S], ALU.add, ALU.mult).then_inc(s["dve"], 1)
                    n[0] += 2
                    v.wait_ge(s["dve"], n[0])
                    lk(V.tensor_tensor(res[:, :], t1[:, :], t2[:, :], ALU.add))
                    v.sem_inc(s["rope"], 1)
                    lk(V.tensor_copy(qkp[:, qk, 0, :], res[:, :]))
                    lk(V.tensor_tensor(t1[:, :], res[:, :], qkp[:, qk, 0, :], ALU.subtract))
                    lk(V.tensor_copy(qkp[:, qk, 1, :], t1[:, :]))
                    V.tensor_tensor(qkp[:, qk, 2, :], t1[:, :], qkp[:, qk, 1, :], ALU.subtract).then_inc(s["parts"], 1)
                    v.wait_ge(s["parts"], 2 * b + qk + 1)
                V.tensor_tensor(prod[:, :], qf[:, :], kf[:, :], ALU.mult).then_inc(s["prod_ready"], 1)
                v.wait_ge(s["ld_ps"], b + 1)
                v.wait_ge(s["parts_st"], 16 * 24 * (b + 1))
            if STOP < 2:
                return
            v.sem_inc(s["a_ready"], 1)
            mrow = mx[:, :, :].rearrange("p g (e c) -> p g e c", e=2)
            restart()
            v.wait_ge(s["ld_sb"], B)
            lk(V.memset(pb[3][:, 0:512], 0.0))

            def maxima(i, b):
                k = 0
                nch = 1 if i < 4 else 2
                for h in range(H):
                    for c in range(nch):
                        w = min(512, (i + 1) * P - 512 * c)
                        v.wait_ge(s["max_lg"], mlg(i, b, k) + 1)
                        V.reduce_max(mraw[:, h, c:c + 1], pb[0][:, (k % 2) * 512:(k % 2) * 512 + w], AX.X).then_inc(s["max_red"], 1)
                        k += 1
                v.wait_ge(s["max_red"], mlg(i, b, k))
                if nch == 2:
                    lk(V.tensor_tensor(mfin[:, :], mraw[:, :, 0], mraw[:, :, 1], ALU.max))
                else:
                    lk(V.tensor_copy(mfin[:, :], mraw[:, :, 0]))
                mf = mfin[:, :].rearrange("p (g e) -> p g e", e=2)
                lk(V.tensor_scalar(mrow[:, :, :, KR], mf, -1.0, None, ALU.mult))
                lk(V.scalar_tensor_tensor(mrow[:, :, :, KR + 1], mf, -1.0, mrow[:, :, :, KR], ALU.mult, ALU.subtract))
                eb = esub[:, b, :].rearrange("p (g e) -> p g e", e=2)
                lb = ldg[:, b, i, :].rearrange("p (g e) -> p g e", e=2)
                if i:
                    v.wait_ge(s["es_ready"], i)
                lk(V.tensor_tensor(eb, lb, mrow[:, :, :, KR], ALU.add))
                V.tensor_tensor(eb, eb, mrow[:, :, :, KR + 1], ALU.add).then_inc(s["mx_ready"], 1)

            def shifted_queries(i, b):
                v.wait_ge(s["mT_done"], 4 * i + b + 1)
                V.tensor_tensor(qm[:, :, :].rearrange("p g n -> p (g n)"), qa[:, :, :].rearrange("p g n -> p (g n)"), pb[0][:, :], ALU.add).then_inc(s["qm_ready"], 1)

            def attend_dve(i, b, after):
                restart()
                if after:
                    maxima(*after)
                    shifted_queries(*after)
                v.wait_ge(s["rn_ps"], 4 * i + b + 1)
                V.tensor_copy(rsb[:, b, :, :].rearrange("p (g q) d -> p g q d", g=4), rback[:, :, :, 0:HD + 1]).then_inc(s["r_evac"], 1)
            maxima(0, 0)
            shifted_queries(0, 0)
            for i in range(NI):
                with v.Fori(0, B - 1) as b:
                    attend_dve(i, b, (i, b + 1))
                attend_dve(i, B - 1, (i + 1, 0) if i < NI - 1 else None)
                restart()
                v.wait_ge(s["r_evac"], 4 * (i + 1))
                V.reciprocal(rdn[:, :, :], rsb[:, :, :, HD]).then_inc(s["rd_ready"], 1)
                v.wait_ge(s["es_ready"], i + 1)
                v.wait_ge(s["rd_ready"], i + 1)
                v.wait_ge(s["rdT_ps"], i + 1)
                V.tensor_copy(rdT[:, :], pb[1][0:B * H, 0:P]).then_inc(s["rdT_sb"], 1)
                lk(V.tensor_tensor(rn[:, :, :, :], v_all[:, :, i, :, :], es[:, :, :].unsqueeze(3).broadcast_to([P, B, H, HD]), ALU.mult))
                lk(V.tensor_tensor(rn[:, :, :, :], rn[:, :, :, :], rsb[:, :, :, 0:HD], ALU.add))
                lk(V.tensor_tensor(rn[:, :, :, :], rn[:, :, :, :], rdn[:, :, :].unsqueeze(3).broadcast_to([P, B, H, HD]), ALU.mult))
                if i:
                    v.wait_ge(s["z_st"], 16 * i)
                for e in range(2):
                    lk(V.tensor_copy(zb[:, e, :, :].rearrange("p k i -> p (k i)"), cst[:, C_EYE:C_EYE + NB * NB]))
                v.wait_ge(s["x_ld"], 16 * 16 * (i + 1))
                v.wait_ge(s["r_ld"], 16 * 16 * (i + 1))
                lk(V.tensor_tensor(xb[:, :, :, :], xb[:, :, :, :], rdb[:, :, :].unsqueeze(2).broadcast_to([P, 2, NB, NB]), ALU.mult))
                for j in range(NB - 1):
                    w, u = NB - 1 - j, j + 1
                    lk(V.tensor_tensor(tb[:, :, 0:u, 0:w], xb[:, :, j:j + 1, u:].broadcast_to([P, 2, u, w]),
                                       zb[:, :, 0:u, j:j + 1].broadcast_to([P, 2, u, w]), ALU.mult))
                    ins = V.tensor_tensor(zb[:, :, 0:u, u:], zb[:, :, 0:u, u:], tb[:, :, 0:u, 0:w], ALU.add)
                    if j < NB - 2:
                        lk(ins)
                    else:
                        ins.then_inc(s["z_ready"], 1)
                with v.Fori(0, B // 2) as pair:
                    two = 2 * i + pair
                    restart()
                    for c in range(NC):
                        rows = slice(c * NB, (c + 1) * NB)
                        for m in range(2):
                            b = 2 * pair + m
                            if c == 0:
                                V.tensor_copy(rr[rows, m, :, :], rn[rows, b, :, :]).then_inc(s["rr_ready"], 1)
                            else:
                                v.wait_ge(s["acc_done"], 6 * two + 2 * (c - 1) + m + 1)
                                lk(V.tensor_tensor(rr[rows, m, :, :], pacc[m][rows, :, :], rdn[rows, b, :].unsqueeze(2).broadcast_to([NB, H, HD]), ALU.mult))
                                V.tensor_tensor(rr[rows, m, :, :], rr[rows, m, :, :], rn[rows, b, :, :], ALU.add).then_inc(s["rr_ready"], 1)
                    for m in range(2):
                        v.wait_ge(s["acur"], 8 * two + 7 + m)
                        V.tensor_copy(a_all[:, 2 * pair + m, i, :, 0:HD], acur[:, m, :, :]).then_inc(s["a_ready"], 1)
            if STOP < 3:
                return
            v.sem_inc(s["g_free"], 1)
            with v.Fori(0, NI) as i:
                restart()
                v.wait_ge(s["y_ps"], i + 1)
                lk(V.tensor_tensor(tf[:, :, :].rearrange("p b d -> p b d"), pb[0][:, 512:1024].rearrange("p (b d) -> p b d", b=B), mod[:, :, 2, :], ALU.mult))
                lk(V.tensor_tensor(x1[:, :, :], xs[:, :, i, :], tf[:, :, :], ALU.add))
                for t in range(B):
                    V.bn_stats(st2[:, t, :], x1[:, t, :]).then_inc(s["dve"], 1)
                n[0] += B
                v.wait_ge(s["dve"], n[0])
                for t in range(B):
                    V.bn_aggr(mv2[:, t, :], st2[:, t, :]).then_inc(s["dve"], 1)
                n[0] += B
                v.wait_ge(s["dve"], n[0])
                V.tensor_scalar(rs2[:, :], mv2[:, :, 1], EPS, None, ALU.add).then_inc(s["var2"], 1)
                v.wait_ge(s["sd2"], i + 1)
                lk(V.reciprocal(rs2[:, :], sd2[:, :]))
                for t in range(B):
                    V.tensor_scalar(h2[:, t, :], x1[:, t, :], mv2[:, t, 0:1], rs2[:, t:t + 1], ALU.subtract, ALU.mult).then_inc(s["dve"], 1)
                n[0] += B
                v.wait_ge(s["dve"], n[0])
                lk(V.tensor_tensor(h2[:, :, :], h2[:, :, :], mod[:, :, 4, :], ALU.mult))
                V.tensor_tensor(h2[:, :, :], h2[:, :, :], mod[:, :, 3, :], ALU.add).then_inc(s["h2_ready"], 1)
                for c in range(4):
                    v.wait_ge(s["sg"], 4 * i + c + 1)
                    V.tensor_tensor(hid[:, c, :, :].rearrange("p b n -> p (b n)"), sg[:, c % 2, :], pb[1 + c % 2][:, 512:1024], ALU.mult).then_inc(s["act"], 1)
                for t in range(B):
                    wait_alone(v, "sim_ps", 4 * i + t + 1, "passed_dve")
                    for q in range(2):
                        for h in range(RH):
                            c, e = 2 * q + h // 2, h % 2
                            V.max(sv[:, q, t, h, :], pb[1 + t % 2][:, e * 512 + c * P:e * 512 + (c + 1) * P]).then_inc(s["dve"], 1)
                    n[0] += 8
                    v.wait_ge(s["dve"], n[0])
                    for q in range(2):
                        for h in range(RH):
                            c, e = 2 * q + h // 2, h % 2
                            last = V.max_index(iv[:, q, t, h, :], sv[:, q, t, h, :], pb[1 + t % 2][:, e * 512 + c * P:e * 512 + (c + 1) * P])
                    last.then_inc(s["sim_red"], 1)
                v.wait_ge(s["sim_red"], 4 * i + 4)
                TH = B * RH
                svx = sv[:, 0].rearrange("p t h k -> p (t h) k").unsqueeze(3).broadcast_to([P, TH, TOPK, TOPK])
                svy = sv[:, 1].rearrange("p t h k -> p (t h) k").unsqueeze(2).broadcast_to([P, TH, TOPK, TOPK])
                lk(V.tensor_tensor(allsc[:, :, :, :], svx, svy, ALU.add))
                lk(V.tensor_copy(ivf[:, :, :, :].rearrange("p q t k -> p (q t k)"), iv[:, :, :, :, :].rearrange("p q t h k -> p (q t h k)")))
                for m in range(TH):
                    V.max(scs[:, m, :], allsc[:, m].rearrange("p a c -> p (a c)")).then_inc(s["dve"], 1)
                n[0] += TH
                v.wait_ge(s["dve"], n[0])
                for m in range(TH):
                    V.max_index(pos[:, m, :], scs[:, m, :], allsc[:, m].rearrange("p a c -> p (a c)")).then_inc(s["dve"], 1)
                n[0] += TH
                v.wait_ge(s["dve"], n[0])
                V.tensor_tensor(wsub[:, :, :], scs[:, :, :], scs[:, :, 0:1].broadcast_to([P, TH, TOPK]), ALU.subtract).then_inc(s["sub_ready"], 1)
                pf = pos[:, :, :].rearrange("p m k -> p (m k)")
                lk(V.tensor_scalar(pab[:, 0, :], pf, 3, None, ALU.logical_shift_right))
                lk(V.tensor_scalar(pab[:, 1, :], pf, 7, None, ALU.bitwise_and))
                lk(V.tensor_copy(pabf[:, :, :], pab[:, :, :]))
                for q in range(2):
                    lk(V.tensor_tensor(oh[:, :, :], pabf[:, q, :].unsqueeze(2).broadcast_to([P, TH * TOPK, TOPK]),
                                       cst[:, C_IOTA:C_IOTA + TOPK].unsqueeze(1).broadcast_to([P, TH * TOPK, TOPK]), ALU.is_equal))
                    o4 = oh[:, :, :].rearrange("p (m k) a -> p m k a", k=TOPK)
                    lk(V.tensor_tensor(o4, o4, ivf[:, q].unsqueeze(2).broadcast_to([P, TH, TOPK, TOPK]), ALU.mult))
                    lk(V.reduce_sum(isel[:, q, :], oh[:, :, :], AX.X))
                lk(V.scalar_tensor_tensor(ef[:, :], isel[:, 0, :], float(NKEY), isel[:, 1, :], ALU.mult, ALU.add))
                lk(V.tensor_scalar(ef[:, :], ef[:, :], float(NEXP - 1), None, ALU.min))
                V.tensor_copy(ei[:, :], ef[:, :]).then_inc(s["idx_ready"], 1)
                v.wait_ge(s["ex_ready"], i + 1)
                lk(V.reduce_sum(wsum[:, :], wex[:, :, :], AX.X))
                lk(V.reciprocal(wrs[:, :], wsum[:, :]))
                lk(V.tensor_tensor(wex[:, :, :], wex[:, :, :], wrs[:, :].unsqueeze(2).broadcast_to([P, TH, TOPK]), ALU.mult))
                wf = wex[:, :, :].rearrange("p (t h) k -> p t (h k)", t=B)
                lk(V.scalar_tensor_tensor(coef[:, :, 0:SLOTS - 1], ef[:, :].rearrange("p (t m) -> p t m", t=B), NEXP - 1.5, wf, ALU.is_lt, ALU.mult))
                lk(V.tensor_tensor(wf, wf, coef[:, :, 0:SLOTS - 1], ALU.subtract))
                lk(V.reduce_sum(coef[:, :, SLOTS - 1:SLOTS], wf, AX.X))
                for t in range(B):
                    v.wait_ge(s["gathered"], 16 * 32 * (4 * i + t + 1))
                    lk(V.tensor_tensor(pr[:, :, :], gbuf[:, :, 0:D], h2[:, t:t + 1, :].broadcast_to([P, SLOTS, D]), ALU.mult))
                    V.reduce_sum(wd_s[:, :], pr[:, :, :], AX.X).then_inc(s["dots"], 1)
                    v.wait_ge(s["silu_w"], 4 * i + t + 1)
                    lk(V.tensor_tensor(ws[:, :], ws[:, :], coef[:, t, :], ALU.mult))
                    lk(V.tensor_tensor(pr[:, :, :], gbuf[:, :, D:2 * D], ws[:, :].unsqueeze(2).broadcast_to([P, SLOTS, D]), ALU.mult))
                    v.sem_inc(s["g_free"], 1)
                    lk(V.reduce_sum(er[:, :], pr[:, :, :].rearrange("p k d -> p d k"), AX.X))
                    if t == 0:
                        v.wait_ge(s["mlp_ps"], i + 1)
                    lk(V.tensor_tensor(er[:, :], er[:, :], pb[3][:, t * P:(t + 1) * P], ALU.add))
                    lk(V.tensor_tensor(er[:, :], er[:, :], mod[:, t, 5, :], ALU.mult))
                    V.tensor_tensor(ot[:, :], er[:, :], x1[:, t, :], ALU.add).then_inc(s["out_ready"], 1)
                    v.wait_ge(s["out_st"], 16 * (4 * i + t + 1))


def kernel(**inputs):
    import numpy as np
    import concourse.bacc as _bacc
    from concourse.bass_utils import run_bass_kernel_spmd as _run

    nc = _bacc.Bacc("TRN2", target_bir_lowering=False, num_devices=1)
    names = ["L0_attn_hidden_states", "L0_attn_Wqkv", "L0_attn_bqkv", "L0_attn_Wd", "L0_attn_bd", "L0_ffn_Wq", "L0_ffn_keys",
             "L0_ffn_down_embed", "L0_ffn_up_embed", "L0_ffn_Wg", "L0_ffn_Wu", "L0_ffn_Wd", "L0_c", "L0_wmod"]
    arrays = {n: np.ascontiguousarray(inputs[n]) for n in names}
    arrays["constants"] = constants()
    args = [nc.dram_tensor(n, a.shape, mybir.dt.from_np(a.dtype), kind="ExternalInput").ap() for n, a in arrays.items()]
    args.append(nc.dram_tensor("out", (B, S, D), F32, kind="ExternalOutput").ap())
    adaln_block(nc, *args)
    r = _run(nc, [arrays], core_ids=[0])
    return r.results[0]["out"]
```

```python
import concourse.bass as bass
from concourse import mybir
from contextlib import ExitStack

F32 = mybir.dt.float32
BF16 = mybir.dt.bfloat16
U32 = mybir.dt.uint32
ALU = mybir.AluOpType
ACT = mybir.ActivationFunctionType
AX = mybir.AxisListType

B, S, D = 4, 1024, 128
P = 128
NI = S // P
H, HD = 16, 8
G2 = H // 2
SCALE = HD ** -0.5
EPS = 1e-5
INTER, RH, NKEY, NEXP, TOPK = 512, 4, 128, 2048, 8
HALF = 64
NB = 32
NC = P // NB
KR = 48
SLOTS = RH * TOPK + 1
PIECE = SLOTS // 3
BIG = -1.0e30

C_ID, C_MASK, C_BONES = 0, P, 2 * P
C_COS = C_BONES + H
C_SIN = C_COS + S
C_DZ = C_SIN + S
C_IOTA = C_DZ + HD + 1
C_ALL = C_IOTA + TOPK


def constants():
    import numpy as np
    c = np.zeros((P, C_ALL), np.float32)
    c[:, C_ID:C_ID + P] = np.eye(P)
    c[:, C_MASK:C_MASK + P] = np.triu(np.full((P, P), BIG), 1)
    row = np.arange(P)
    hh, d, g2 = row // 64, row // 8 % 8, row % 8
    c[row, C_BONES + 2 * g2 + hh] = 1.0
    t = np.arange(S, dtype=np.float32)
    cos, sin = np.cos(t), np.sin(t)
    c[:, C_COS:C_COS + S] = np.where(d[:, None] < 2, cos[None], 1.0)
    c[:, C_SIN:C_SIN + S] = np.where(d[:, None] == 0, -sin[None], np.where(d[:, None] == 1, sin[None], 0.0))
    c[:, C_DZ + HD] = 1.0
    c[:, C_IOTA:C_IOTA + TOPK] = np.arange(TOPK)
    return c


def adaln_block(nc, x, wqkv, bqkv, wd, bd, wq, keys, down, up, wg, wu, wd2, cc, wmod, cst_in, out):
    ctx = ExitStack()
    with ctx:
        def sb(name, shape, dt=F32, at=ctx):
            return at.enter_context(nc.sbuf_tensor(name, shape, dt))

        def sem(name):
            return ctx.enter_context(nc.semaphore(name))

        def dram(name, shape, dt):
            return nc.dram_tensor(name, shape, dt, kind="Internal").ap()

        qs_d = dram("qs_d", [B, 2, KR, G2, S], BF16)
        ks_d = dram("ks_d", [B, 2, KR, G2, S], BF16)
        ed_d = dram("ed_d", [2, B, P, G2, 2, P], F32)
        rd_d = dram("rd_d", [B, NC, H, NB], F32)
        z_d = dram("z_d", [P, 2, NB, NB], F32)
        table = dram("table", [NEXP, 2 * D], F32)

        cst = sb("cst", [P, C_ALL])
        xs = sb("xs", [P, B, NI, D])
        mod = sb("mod", [P, B, 6, D])
        wT = sb("wT", [P, 24, D])
        bdrow = sb("bdrow", [1, D])
        ones1 = sb("ones1", [1, P])
        a_all = sb("a_all", [P, B, NI, H, HD + 1])
        ident = cst[:, C_ID:C_ID + P]

        pb = [ctx.enter_context(nc.psum_tensor(f"pb{i}", [P, 1024], F32)) for i in range(4)]

        names = (
            "w_in", "tab_in", "c_ready", "wt_ps", "wt_sb", "silu_c", "scb", "mod_ps", "mod_sb", "setup_dve", "pool_c", "bias_ps",
            "h_ready", "hT_ps", "hT_sb", "var_ready", "sd_ready", "proj", "rope", "parts", "parts_st", "prod_ready",
            "ld_ps", "ld_sb", "v_ps", "v_sb",
            "m_ld", "kd_ld", "ke_ld", "ke2_ld", "q_ld", "max_lg", "max_red", "mx_ready", "mT_done", "qm_ready", "e_lg", "exp_done",
            "av_done", "ed_masked", "ed_st", "ast_ready", "ast2_ready", "ast3_ready", "r_done", "rT_sb", "rn_ps", "r_evac",
            "rd_ready", "rdT_ps", "rdT_sb", "rd_st", "x_ld", "r_ld", "es_ready", "z_ready", "z_st",
            "vt_ld", "rr_ready", "px_done", "acur", "acc_done", "a_ready",
            "ac_ready", "at_ps", "at_sb", "y_ps", "h2_ready", "var2", "sd2", "h2T_ps", "h2T_sb", "gu_ps", "sg", "act",
            "mlp_ps", "q_ps", "q_sb", "sim_ps", "sim_red", "sub_ready", "ex_ready", "idx_ready",
            "gathered_even", "gathered_odd", "g_clear", "dots", "silu_w", "wc_ready", "pu_ready", "pu_used", "g_free",
            "out_ready", "out_even", "out_odd",
            "dve", "passed_dve", "passed_pe", "passed_pool")
        s = {n: sem(n) for n in names}

        def link(eng, ins, own, count):
            count[0] += 1
            ins.then_inc(own, 1)
            eng.wait_ge(own, count[0])

        def run(parts):
            for _ in parts:
                pass

        def wait_alone(eng, what, value, passed):
            eng.wait_ge(s[what], value)
            eng.sem_inc(s[passed], 1)

        att = ExitStack()
        km = sb("km", [P, G2, S], BF16, at=att)
        ke = sb("ke", [P, G2, S], BF16, at=att)
        kd = sb("kd", [P, G2, P], BF16, at=att)
        qa = sb("qa", [P, G2, P], BF16, at=att)
        mx = sb("mx", [P, G2, P], BF16, at=att)
        qm = sb("qm", [P, G2, P], BF16, at=att)
        mraw = sb("mraw", [P, H, 2], at=att)
        mfin = sb("mfin", [P, H], at=att)
        et = sb("et", [P, 2, 8, P], at=att)
        ast = sb("ast", [P, NI - 1, H, HD + 1], at=att)
        v_all = sb("v_all", [P, B, NI, H, HD], at=att)
        ldg = sb("ldg", [P, B, NI, H], at=att)
        identb = sb("identb", [P, P], BF16, at=att)
        maskb = sb("maskb", [P, P], BF16, at=att)
        prep = ExitStack()
        wnat = sb("wnat", [P, 24, D], at=prep)
        wrow = sb("wrow", [1, 3 * D], at=prep)
        brow = sb("brow", [1, 4, P], at=prep)
        wp = sb("wp", [P, 4, P], at=prep)
        bcol = sb("bcol", [P, 4], at=prep)
        cT = sb("cT", [P, B], at=prep)
        sc = sb("sc", [P, B], at=prep)
        scb = sb("scb", [P, B, P], at=prep)
        wm = sb("wm", [P, 6 * D], at=prep)
        tmpm = sb("tmpm", [P, B, D], at=prep)
        st = sb("st", [P, NI, 6], at=prep)
        mv = sb("mv", [P, NI, 2], at=prep)
        sd = sb("sd", [P, NI], at=prep)
        rs = sb("rs", [P, NI], at=prep)
        hn = sb("hn", [P, NI, D], at=prep)
        hT = sb("hT", [P, S], at=prep)
        t1 = sb("t1", [P, S], at=prep)
        t2 = sb("t2", [P, S], at=prep)
        qf = sb("qf", [P, S], at=prep)
        kf = sb("kf", [P, S], at=prep)
        prod = sb("prod", [P, S], at=prep)
        qkp = sb("qkp", [P, 2, 3, S], BF16, at=prep)

        prep.close()
        esub = sb("esub", [P, B, H], at=att)
        es = sb("es", [P, B, H], at=att)

        ed = sb("ed", [P, G2, 2, P], at=att)

        rsb = sb("rsb", [P, B, H, HD + 1], at=att)
        rdn = sb("rdn", [P, B, H], at=att)
        rn = sb("rn", [P, B, H, HD], at=att)
        rdT = sb("rdT", [B * H, P], at=att)
        xb = cst[:, C_COS:C_COS + 2 * NB * NB].rearrange("p (e j i) -> p e j i", e=2, j=NB)
        rdb = sb("rdb", [P, 2, NB], at=att)
        zb = sb("zb", [P, 2, NB, NB], at=att)
        ztmp = sb("ztmp", [P, 2 * NB * NB], at=att)
        tb = ztmp[:, :].rearrange("p (e k i) -> p e k i", e=2, k=NB)
        vtb = ztmp[:, :].rearrange("p (b h i) -> p b h i", b=B, h=H)
        edb = sb("edb", [P, B, H, P], at=att)
        rts = sb("rts", [P, 4, P], at=att)
        rr = sb("rr", [P, B, H, HD], at=att)
        acur = sb("acur", [P, B, H, HD], at=att)
        att.close()

        ffn = ctx
        pr = sb("pr", [P, PIECE, D], at=ffn)
        pu = sb("pu", [P, 2, PIECE, D], at=ffn)
        h2 = sb("h2", [P, 2, B, D], at=ffn)
        h2T = sb("h2T", [P, B, P], at=ffn)
        st2 = sb("st2", [P, B, 6], at=ffn)
        mv2 = sb("mv2", [P, B, 2], at=ffn)
        sd2 = sb("sd2t", [P, B], at=ffn)
        rs2 = sb("rs2", [P, B], at=ffn)
        sg = sb("sgt", [P, 2, 512], at=ffn)
        qT = sb("qT", [P, 4, B, P], at=ffn)
        sv = sb("sv", [P, 2, B, RH, TOPK], at=ffn)
        iv = sb("iv", [P, 2, B, RH, TOPK], U32, at=ffn)
        ivf = sb("ivf", [P, 2, B * RH, TOPK], at=ffn)
        scs = sb("scs", [P, B * RH, TOPK], at=ffn)
        pos = sb("pos", [P, B * RH, TOPK], U32, at=ffn)
        pab = sb("pab", [P, 2, B * RH * TOPK], U32, at=ffn)
        pabf = sb("pabf", [P, 2, B * RH * TOPK], at=ffn)
        isel = sb("isel", [P, 2, B * RH * TOPK], at=ffn)
        ef = sb("ef", [P, B * RH * TOPK], at=ffn)
        ei = sb("ei", [P, 2, B * RH * TOPK], U32, at=ffn)
        wsub = sb("wsub", [P, B * RH, TOPK], at=ffn)
        wex = sb("wex", [P, B * RH, TOPK], at=ffn)
        wsum = sb("wsum", [P, B * RH], at=ffn)
        wrs = sb("wrs", [P, B * RH], at=ffn)
        coef = sb("coef", [P, 2, B, SLOTS], at=ffn)
        wd_s = sb("wd_s", [P, SLOTS], at=ffn)
        ws = sb("ws", [P, SLOTS], at=ffn)
        wc = sb("wc", [P, 2, SLOTS], at=ffn)
        ot = sb("ot", [P, 2, D], at=ffn)
        grid = sb("grid", [P, B * RH * TOPK * TOPK], at=ffn)
        gbuf = sb("gbuf", [P, 2, SLOTS, 2 * D], at=ffn)
        tf = sg[:, 0, :].rearrange("p (b d) -> p b d", b=B)
        ac = sg[:, 1, :].rearrange("p (b d) -> p b d", b=B)
        aT = qT[:, 0, :, :]
        hid = cst[:, C_COS:C_COS + INTER * B].rearrange("p (c b n) -> p c b n", c=4, b=B)
        allsc = grid[:, :].rearrange("p (m a c) -> p m a c", a=TOPK, c=TOPK)
        oh = grid[:, :].rearrange("p (m a) -> p m a", a=TOPK)

        def chunks_before(i):
            return 4 * sum(2 * (j + 1) for j in range(i))

        def chunk(i, b, n):
            return chunks_before(i) + b * (2 * (i + 1)) + n

        def max_parts(i):
            together = max(1, 512 // ((i + 1) * P))
            return [(range(h + hh, h + hh + 2 * together, 2), c0) for h in range(0, H, 2 * together) for hh in range(2)
                    for c0 in range(0, (i + 1) * P, 512)]

        def mcount(i):
            return len(max_parts(i))

        def mlg(i, b, n):
            return 4 * sum(mcount(j) for j in range(i)) + b * mcount(i) + n

        def off(i, b, n):
            return 4 * sum(2 * j for j in range(i)) + b * (2 * i) + n

        def blocks(i, n):
            res = []
            for k in range(4):
                for hh in range(2):
                    g2, j = (4 * n + k, i) if n < 2 else (4 * (n % 2) + k, (n - 2) // 2)
                    res.append((hh * 4 + k, g2, hh, j))
            return res

        rT = pb[3][:, 0:512].rearrange("p (g n) -> p g n", g=4)
        rback = pb[3][:, 512:1024].rearrange("p (g q d) -> p g q d", g=4, q=4)
        solver = [pb[1 + m // 2][:, (m % 2) * 512:(m % 2) * 512 + 2 * D].rearrange("p (w h d) -> p w h d", w=2, h=H) for m in range(B)]
        px = [t[:, 0] for t in solver]
        pacc = [t[:, 1] for t in solver]

        gathered, out_st = ("gathered_even", "gathered_odd"), ("out_even", "out_odd")

        def run_units(eng, unit):
            with eng.Fori(0, NI // 2 - 1) as two:
                unit(2 * two, 0, True)
                unit(2 * two + 1, 1, True)
            unit(NI - 2, 0, True)
            unit(NI - 1, 1, False)

        block = ctx.enter_context(nc.Block())
        NSETUP_IN = [0]

        @block.sync
        def _(sp):
            w = s["w_in"]

            def ld(dst, src):
                sp.dma_start(dst, src).then_inc(w, 16)
                NSETUP_IN[0] += 1
            ld(cst[:, :], cst_in)
            ld(wnat[:, 0:3, :], wqkv.rearrange("(t p) d -> p t d", p=P))
            ld(wnat[:, 3, :], wd)
            ld(wnat[:, 4:8, :], wq.rearrange("(t p) d -> p t d", p=P))
            ld(wnat[:, 8:12, :], wg.rearrange("(t p) d -> p t d", p=P))
            ld(wnat[:, 12:16, :], wu.rearrange("(t p) d -> p t d", p=P))
            ld(wnat[:, 16:20, :], wd2.rearrange("p (t d) -> p t d", d=P))
            kn = wnat[:, 20:24, :].rearrange("k (q m) (e n) -> k q m e n", q=2, e=2)
            for h in range(RH):
                ld(kn[:, :, h // 2, h % 2, :], keys[h])
            ld(wrow[:, :], bqkv.rearrange("(a n) -> a n", a=1))
            ld(bdrow[:, :], bd.rearrange("(a n) -> a n", a=1))
            with nc.allow_non_contiguous_dma(reason="512 elements"):
                ld(cT[:, :], cc.rearrange("b k -> k b"))
            ld(wm[:, :], wmod)
            for b in range(B):
                ld(xs[:, b, :, :], x[b].rearrange("(i p) d -> p i d", p=P))
            sp.dma_start(table[:, 0:D], down).then_inc(s["tab_in"], 16)
            sp.dma_start(table[:, D:2 * D], up).then_inc(s["tab_in"], 16)
            sp.sem_inc(s["parts_st"], 16)
            with sp.Fori(0, B) as b:
                for qk, dst, order in ((0, qs_d, (0, 0, 1, 1, 0, 2)), (1, ks_d, (0, 1, 0, 1, 2, 0))):
                    sp.wait_ge(s["parts"], 2 * b + qk + 1)
                    for hh in range(2):
                        for r, part in enumerate(order):
                            sp.dma_start(dst[b, hh, r * HD:(r + 1) * HD, :, :].rearrange("d g s -> (d g) s"),
                                         qkp[64 * hh:64 * hh + 64, qk, part, :]).then_inc(s["parts_st"], 16)
            sp.wait_ge(s["parts_st"], 16 * 24 * B + 16)
            sp.wait_ge(s["pool_c"], 1)
            sp.sem_inc(s["ed_st"], 16)
            steps = [(i, b) for i in range(NI) for b in range(B)]

            def load_km(i, b):
                for hh in range(2):
                    sp.dma_start(km[64 * hh:64 * hh + KR, :, 0:(i + 1) * P], ks_d[b, hh, :, :, 0:(i + 1) * P]).then_inc(s["m_ld"], 16)

            def load_qa(i, b):
                for hh in range(2):
                    sp.dma_start(qa[64 * hh:64 * hh + KR, :, :], qs_d[b, hh, :, :, i * P:(i + 1) * P]).then_inc(s["q_ld"], 16)

            def load_kd(i, b):
                for hh in range(2):
                    sp.dma_start(kd[64 * hh:64 * hh + KR, :, :], ks_d[b, hh, :, :, i * P:(i + 1) * P]).then_inc(s["kd_ld"], 16)

            def load_ke(i, b, part):
                half = (i + 1) // 2
                j0, j1 = ((0, half), (half, i))[part]
                for hh in range(2):
                    sp.dma_start(ke[64 * hh:64 * hh + KR, :, j0 * P:j1 * P], ks_d[b, hh, :, :, j0 * P:j1 * P]
                                 ).then_inc(s[("ke_ld", "ke2_ld")[part]], 16)
            load_km(0, 0)
            load_qa(0, 0)
            load_kd(0, 0)
            sp.wait_ge(s["mx_ready"], 1)
            load_km(0, 1)
            def start_of_step(n):
                i, b = steps[n]
                if n + 1 < len(steps):
                    sp.wait_ge(s["qm_ready"], n + 1)
                    load_qa(*steps[n + 1])
                if i > (i + 1) // 2:
                    sp.wait_ge(s["e_lg"], chunk(i, b, 0))
                    load_ke(i, b, 1)
                if n + 1 < len(steps):
                    sp.wait_ge(s["e_lg"], chunk(i, b, 1) + 1)
                    load_kd(*steps[n + 1])

            def diagonal_to_inversion(i, b):
                sp.wait_ge(s["ed_st"], 16 * (4 * i + b + 2))
                for c in range(NC):
                    sp.dma_start(xb[b * 32 + c * 8:b * 32 + c * 8 + 8, :, :, :],
                                 ed_d[i % 2, b, c * NB:(c + 1) * NB, :, :, c * NB:(c + 1) * NB].rearrange("j g e i -> g e j i")
                                 ).then_inc(s["x_ld"], 16)
            for n, (i, b) in enumerate(steps):
                after = steps[n + 1] if n + 1 < len(steps) else None
                if b or not i:
                    start_of_step(n)
                if b:
                    diagonal_to_inversion(i, b - 1)
                sp.wait_ge(s["ed_masked"], n + 1)
                sp.dma_start(ed_d[i % 2, b], ed[:, :, :, :]).then_inc(s["ed_st"], 16)
                if b == B - 1:
                    diagonal_to_inversion(i, b)
                if after:
                    if after[0]:
                        sp.wait_ge(s["e_lg"], chunk(i, b, 2 + 2 * min((after[0] + 1) // 2, i) - 1) + 1)
                        load_ke(*after, 0)
                    if n + 2 < len(steps):
                        sp.wait_ge(s["mx_ready"], n + 2)
                        load_km(*steps[n + 2])
                if b == B - 1:
                    sp.wait_ge(s["rdT_sb"], i + 1)
                    for bb in range(B):
                        sp.dma_start(rd_d[bb].rearrange("c h n -> h c n"), rdT[bb * H:(bb + 1) * H, :].rearrange("h (c n) -> h c n", c=NC)).then_inc(s["rd_st"], 16)
                    sp.wait_ge(s["rd_st"], 16 * B * (i + 1))
                    sp.dma_start(rdb[:, :, :].rearrange("p e n -> p (e n)"), rd_d.rearrange("b c (g e) n -> (b c g) (e n)", e=2)).then_inc(s["r_ld"], 16)
                    if after:
                        start_of_step(n + 1)
                    sp.wait_ge(s["a_ready"], 4 * i + 1)
                    for bb in range(B):
                        sp.dma_start(edb[:, bb, :, :], ed_d[i % 2, bb].rearrange("j g e i -> j (g e) i")).then_inc(s["vt_ld"], 16)
                    sp.wait_ge(s["z_ready"], i + 1)
                    sp.dma_start(z_d, zb[:, :, :, :]).then_inc(s["z_st"], 16)
                    sp.wait_ge(s["z_st"], 16 * (i + 1))
                    zv = z_d.rearrange("(b c g) e k i -> b c k (g e) i", b=B, c=NC)
                    for bb in range(B):
                        for c in range(NC):
                            sp.dma_start(vtb[c * NB:(c + 1) * NB, bb, :, :], zv[bb, c]).then_inc(s["vt_ld"], 16)
            sp.wait_ge(s["tab_in"], 32)
            sp.wait_ge(s["pool_c"], 2)
            sp.wait_ge(s["g_clear"], 1)
            for w in range(2):
                sp.dma_start(gbuf[:, w, SLOTS - 1, :], table[NEXP - 1:NEXP, :].broadcast_to([P, 2 * D])).then_inc(s["tab_in"], 16)
            sp.sem_inc(s["out_even"], 16)
            sp.sem_inc(s["out_odd"], 16)
            with sp.Fori(0, NI) as i:
                for t in range(B):
                    sp.wait_ge(s["out_ready"], 4 * i + t + 1)
                    sp.dma_start(out[t, bass.ds(i * P, P), :], ot[:, t % 2, :]).then_inc(s[out_st[t % 2]], 16)
            for w in range(2):
                sp.wait_ge(s[out_st[w]], 16 * (B * NI // 2 + 1))

        @block.gpsimd
        def _(g):
            nc.gpsimd.memset(ones1[:, :], 1.0).then_inc(s["c_ready"], 1)
            nc.gpsimd.memset(km[:, :, :], 1.0).then_inc(s["c_ready"], 1)
            nc.gpsimd.memset(ke[:, :, :], 1.0).then_inc(s["c_ready"], 1)
            nc.gpsimd.memset(kd[:, :, :], 1.0).then_inc(s["c_ready"], 1)
            nc.gpsimd.memset(qa[:, :, :], 0.0).then_inc(s["c_ready"], 1)
            nc.gpsimd.memset(mx[:, :, :], 0.0).then_inc(s["c_ready"], 1)
            nc.gpsimd.memset(a_all[:, :, :, :, :], 1.0).then_inc(s["c_ready"], 1)
            g.wait_ge(s["c_ready"], 7)
            g.sem_inc(s["pool_c"], 1)
            zero = g.to_reg(0.0)
            last_gathered = g.to_reg(NEXP - 2)
            for i in range(NI):
                half = (i + 1) // 2

                def copy_a(b, j0, j1, done):
                    nc.gpsimd.tensor_copy(ast[:, j0:j1, :, :], a_all[:, b, j0:j1, :, :]).then_inc(s[done], 1)

                def mask(b):
                    wait_alone(g, "exp_done", chunk(i, b, 1) + 1 + 2, "passed_pool")
                    nc.gpsimd.affine_select(out=ed[:, :, :, :], in_=ed[:, :, :, :], compare_op=ALU.is_ge, fill=zero, base=0,
                                            pattern=[[0, 2], [0, G2], [1, P]], channel_multiplier=-1).then_inc(s["ed_masked"], 1)
                if i:
                    wait_alone(g, "r_done", 4 * i, "passed_pool")
                    if i > 1:
                        g.wait_ge(s["a_ready"], 4 * (i - 1) + 1)
                        copy_a(0, 0, half, "ast_ready")
                    if i > 3:
                        copy_a(0, half, i - 1, "ast2_ready")
                    mask(0)
                    g.wait_ge(s["a_ready"], 4 * i + 1)
                    copy_a(0, i - 1, i, "ast_ready" if i == 1 else "ast2_ready" if i < 4 else "ast3_ready")
                with g.Fori(1 if i else 0, B) as b:
                    step = 4 * i + b
                    if i:
                        g.wait_ge(s["av_done"], off(i, b, 0) - 2 * (i - half) + 2)
                        copy_a(b, 0, half, "ast_ready")
                        if i > half:
                            wait_alone(g, "r_done", step, "passed_pool")
                            copy_a(b, half, i, "ast2_ready")
                    mask(b)
            g.wait_ge(s["a_ready"], 4 * NI + 1)
            nc.gpsimd.memset(gbuf[:, 0, :, :], 0.0).then_inc(s["pool_c"], 1)
            g.wait_ge(s["tab_in"], 64)
            with g.Fori(0, NI // 2) as two:
                for u in range(2):
                    i = 2 * two + u
                    wait_alone(g, "idx_ready", i + 1, "passed_pool")
                    for t in range(B):
                        wait_alone(g, "g_free", 4 * i + t + 1, "passed_pool")
                        for k in range(SLOTS - 1):
                            nc.gpsimd.indirect_dma_start(gbuf[:, t % 2, k, :], None, table,
                                                         bass.IndirectOffsetOnAxis(ei[:, u, t * 32 + k:t * 32 + k + 1], 0),
                                                         bounds_check=last_gathered, oob_is_err=False).then_inc(s[gathered[t % 2]], 16)

        @block.scalar
        def _(a):
            a.wait_ge(s["w_in"], 16 * NSETUP_IN[0])
            nc.scalar.activation(sc[:, :], cT[:, :], ACT.Silu).then_inc(s["silu_c"], 1)
            for n in range(6):
                a.wait_ge(s["wt_ps"], n + 1)
                nc.scalar.activation(wT[:, 4 * n:4 * n + 4, :], pb[n % 4][:, 0:512].rearrange("p (t d) -> p t d", d=D), ACT.Copy).then_inc(s["wt_sb"], 1)
            for b in range(B):
                a.wait_ge(s["mod_ps"], b + 1)
                nc.scalar.activation(mod[:, b, :, :].rearrange("p m d -> p (m d)"), pb[b][:, 0:768], ACT.Copy).then_inc(s["mod_sb"], 1)

            def deviations(b):
                a.wait_ge(s["var_ready"], b + 1)
                nc.scalar.activation(sd[:, :], rs[:, :], ACT.Sqrt).then_inc(s["sd_ready"], 1)

            def turned(b):
                a.wait_ge(s["hT_ps"], b + 1)
                nc.scalar.activation(hT[:, :], pb[0][:, :], ACT.Copy).then_inc(s["hT_sb"], 1)

            def values(b, more):
                if more:
                    deviations(b + 1)
                a.wait_ge(s["v_ps"], b + 1)
                nc.scalar.activation(v_all[:, b, :, :, :].rearrange("p i h d -> p (i h d)"), pb[0][:, :], ACT.Copy).then_inc(s["v_sb"], 1)
                if more:
                    turned(b + 1)
                a.wait_ge(s["ld_ps"], b + 1)
                nc.scalar.activation(ldg[:, b, :, :].rearrange("p i h -> p (i h)"), pb[3][:, 0:NI * H], ACT.Copy).then_inc(s["ld_sb"], 1)
            deviations(0)
            turned(0)
            with a.Fori(0, B - 1) as b:
                values(b, True)
            values(B - 1, False)
            a.sem_inc(s["exp_done"], 2)
            def exps(i, b, split=False):
                step = 4 * i + b
                for n in range(2 * (i + 1)):
                    if split and n == 2 * i:
                        yield
                    a.wait_ge(s["e_lg"], chunk(i, b, n) + 1)
                    src = pb[1 + n % 2][:, :].rearrange("p (e k i) -> p e k i", e=2, k=4)
                    if n < 2:
                        if n == 0:
                            a.wait_ge(s["ed_st"], 16 * (step + 1))
                        dst = ed[:, 4 * n:4 * n + 4, :, :].rearrange("p k e i -> p e k i")
                    else:
                        a.wait_ge(s["av_done"], off(i, b, n - 2) + 1)
                        dst = et[:, n % 2, :, :].rearrange("p (e k) i -> p e k i", e=2)
                    nc.scalar.activation(dst, src, ACT.Exp, scale=SCALE).then_inc(s["exp_done"], 1)
                a.wait_ge(s["r_done"], step + 1)
                nc.scalar.activation(rts[:, :, :].rearrange("p g n -> p (g n)"), pb[3][:, 0:512], ACT.Copy).then_inc(s["rT_sb"], 1)
            def nothing(k):
                pass

            def attention_out(i, between):
                nc.scalar.activation(ac.rearrange("p b (h d) -> p b h d", d=HD), a_all[:, :, i, :, 0:HD], ACT.Copy).then_inc(s["ac_ready"], 1)
                between(0)
                a.wait_ge(s["at_ps"], i + 1)
                nc.scalar.activation(aT.rearrange("p b n -> p (b n)"), pb[0][:, 0:512], ACT.Copy).then_inc(s["at_sb"], 1)
                between(1)
                a.wait_ge(s["var2"], i + 1)
                nc.scalar.activation(sd2[:, :], rs2[:, :], ACT.Sqrt).then_inc(s["sd2"], 1)
                between(2)
                a.wait_ge(s["h2T_ps"], i + 1)
                nc.scalar.activation(h2T[:, :, :].rearrange("p b n -> p (b n)"), pb[0][:, 0:512], ACT.Copy).then_inc(s["h2T_sb"], 1)

            def gates_queries(i, between):
                for c in range(4):
                    a.wait_ge(s["gu_ps"], 4 * i + c + 1)
                    if c >= 2:
                        a.wait_ge(s["act"], 4 * i + c - 1)
                    nc.scalar.activation(sg[:, c % 2, :], pb[1 + c % 2][:, 0:512], ACT.Silu).then_inc(s["sg"], 1)
                    if c < 3:
                        between(c)
                for c in range(4):
                    a.wait_ge(s["q_ps"], 4 * i + c + 1)
                    nc.scalar.activation(qT[:, c, :, :].rearrange("p b n -> p (b n)"), pb[0][:, (c % 2) * 512:(c % 2) * 512 + 512], ACT.Copy).then_inc(s["q_sb"], 1)

            def selection(i, between):
                for k in range(3):
                    between(k)
                a.wait_ge(s["sub_ready"], i + 1)
                nc.scalar.activation(wex[:, :, :], wsub[:, :, :], ACT.Exp).then_inc(s["ex_ready"], 1)

            first = None
            for i in range(NI):
                if i:
                    run(first)
                with a.Fori(1 if i else 0, B - 1) as b:
                    run(exps(i, b))
                a.wait_ge(s["mx_ready"], 4 * (i + 1))
                nc.scalar.activation(es[:, :, :], esub[:, :, :], ACT.Exp, scale=SCALE).then_inc(s["es_ready"], 1)
                run(exps(i, B - 1))
                if i < NI - 1:
                    first = exps(i + 1, 0, True)
                    next(first)
                else:
                    attention_out(0, nothing)
                    gates_queries(0, nothing)
                for c in range(NC):
                    rows = slice(c * NB, (c + 1) * NB)
                    for m in range(B):
                        a.wait_ge(s["px_done"], 16 * i + 4 * c + m + 1)
                        if c == 0:
                            a.wait_ge(s["a_ready"], 4 * i + 1)
                        nc.scalar.activation(acur[rows, m, :, :], px[m][rows, :, :], ACT.Copy).then_inc(s["acur"], 1)
                    if i == NI - 1 and c == 0:
                        selection(0, nothing)

            def unit(i, u, more):
                for t in range(B):
                    a.wait_ge(s["dots"], 4 * i + t + 1)
                    nc.scalar.activation(ws[:, :], wd_s[:, :], ACT.Silu).then_inc(s["silu_w"], 1)

                    def weigh(k):
                        if k == 0:
                            a.wait_ge(s["wc_ready"], 4 * i + t + 1)
                        a.wait_ge(s["pu_used"], 3 * (4 * i + t) + k + 1)
                        for m in range(PIECE):
                            slot = k * PIECE + m
                            last = nc.scalar.activation(pu[:, (3 * t + k) % 2, m, :], gbuf[:, t % 2, slot, D:2 * D], ACT.Copy,
                                                        scale=wc[:, t % 2, slot:slot + 1])
                        last.then_inc(s["pu_ready"], 1)
                    if more and t == 0:
                        attention_out(i + 1, weigh)
                        gates_queries(i + 1, nothing)
                    elif more and t == 2:
                        selection(i + 1, weigh)
                    else:
                        for k in range(3):
                            weigh(k)
            a.sem_inc(s["g_free"], 2)
            run_units(a, unit)

        @block.tensor
        def _(pe):
            mm = nc.tensor.matmul
            pe.wait_ge(s["w_in"], 16 * NSETUP_IN[0])
            for n in range(6):
                if n >= 4:
                    pe.wait_ge(s["wt_sb"], n - 3)
                for t in range(4):
                    last = mm(pb[n % 4][:, t * P:(t + 1) * P], wnat[:, 4 * n + t, :], ident, start=True, stop=True)
                last.then_inc(s["wt_ps"], 1)
            pe.wait_ge(s["scb"], 1)
            pe.wait_ge(s["wt_sb"], 6)
            for b in range(B):
                mm(pb[b][:, 0:512], scb[:, b, :], wm[:, 0:512], start=True, stop=True)
                mm(pb[b][:, 512:768], scb[:, b, :], wm[:, 512:768], start=True, stop=True).then_inc(s["mod_ps"], 1)
            pe.wait_ge(s["c_ready"], 7)
            pe.wait_ge(s["setup_dve"], 1)
            pe.wait_ge(s["mod_sb"], B)
            for n in range(4):
                last = mm(pb[3][:, n:n + 1], brow[0:1, n, :], ones1[0:1, 0:1], start=True, stop=True)
            last.then_inc(s["bias_ps"], 1)
            def turn(b):
                pe.wait_ge(s["h_ready"], b + 1)
                for t in range(NI):
                    last = mm(pb[0][:, t * P:(t + 1) * P], hn[:, t, :], ident, start=True, stop=True)
                last.then_inc(s["hT_ps"], 1)

            def project(b, more):
                pe.wait_ge(s["hT_sb"], b + 1)
                for t in range(NI):
                    mm(pb[0][:, t * P:(t + 1) * P], hT[:, t * P:(t + 1) * P], wT[:, 2, :], start=True, stop=False)
                    last = mm(pb[0][:, t * P:(t + 1) * P], ones1[0:1, :], wrow[0:1, 2 * D:3 * D], start=False, stop=True)
                last.then_inc(s["v_ps"], 1)
                for qk in range(2):
                    if qk:
                        pe.wait_ge(s["rope"], 2 * b + 1)
                    for w in range(2):
                        for half in range(2):
                            last = mm(pb[1 + w][:, half * 512:(half + 1) * 512], wp[:, 2 * qk + w, :], hT[:, half * 512:(half + 1) * 512], start=True, stop=True)
                    last.then_inc(s["proj"], 1)
                pe.wait_ge(s["v_sb"], b + 1)
                if more:
                    turn(b + 1)
                pe.wait_ge(s["prod_ready"], b + 1)
                for t in range(NI):
                    last = mm(pb[3][:, t * H:(t + 1) * H], prod[:, t * P:(t + 1) * P], cst[:, C_BONES:C_BONES + H], start=True, stop=True)
                last.then_inc(s["ld_ps"], 1)
                pe.wait_ge(s["ld_sb"], b + 1)
            turn(0)
            with pe.Fori(0, B - 1) as b:
                project(b, True)
            project(B - 1, False)
            pe.sem_inc(s["av_done"], 2)

            def max_units(i, b):
                for n, (heads, c0) in enumerate(max_parts(i)):
                    w = min(512, (i + 1) * P - c0)
                    if n == 0:
                        pe.wait_ge(s["m_ld"], 32 * (4 * i + b + 1))
                        pe.wait_ge(s["q_ld"], 32 * (4 * i + b + 1))
                    if n >= 2:
                        pe.wait_ge(s["max_red"], mlg(i, b, n - 1))
                    for m, h in enumerate(heads):
                        g2, hh = h // 2, h % 2
                        place = pb[0][:, (n % 2) * 512 + m * w:(n % 2) * 512 + (m + 1) * w]
                        last_block = c0 + w == (i + 1) * P
                        last = mm(place, qa[64 * hh:64 * hh + KR, g2, :], km[64 * hh:64 * hh + KR, g2, c0:c0 + w],
                                  start=True, stop=not last_block)
                        if last_block:
                            last = mm(place[:, w - P:w], identb[:, :], maskb[:, :], start=False, stop=True)
                    last.then_inc(s["max_lg"], 1)
                    yield

            def turn_maxima(i, b):
                pe.wait_ge(s["mx_ready"], 4 * i + b + 1)
                for g2 in range(G2):
                    last = mm(pb[0][:, g2 * P:(g2 + 1) * P], mx[:, g2, :], identb[:, :], start=True, stop=True)
                last.then_inc(s["mT_done"], 1)

            def attend(i, b, after, split=False):
                step = 4 * i + b
                total = 2 * (i + 1)
                half = (i + 1) // 2
                units = max_units(*after) if after else iter(())
                todo = mcount(after[0]) if after and not split else 0
                given = [0]

                def spread(phase):
                    share = min(todo, todo * (phase + 1) // (2 * total - 2))
                    while given[0] < share:
                        next(units)
                        given[0] += 1
                started = set()

                def multiply(n):
                    if n >= 2:
                        pe.wait_ge(s["exp_done"], chunk(i, b, n) + 3)
                        if n == 2:
                            pe.wait_ge(s["ast_ready"], 4 * (i - 1) + b + 1)
                        if n == 2 + 2 * half:
                            pe.wait_ge(s["ast2_ready"], 4 * (i - 2) + b + 1)
                    elif n == 0:
                        pe.wait_ge(s["ed_masked"], step + 1)
                    for k, g2, hh, j in blocks(i, n):
                        h = 2 * g2 + hh
                        q = h % 4
                        rhs = et[:, n % 2, k, :] if n >= 2 else ed[:, g2, hh, :]
                        lhs = ast[:, j, h, :] if n >= 2 else cst[:, C_DZ:C_DZ + HD + 1]
                        last = mm(rT[32 * q:32 * q + HD + 1, h // 4, :], lhs, rhs, start=q not in started, stop=True, skip_group_check=True)
                        started.add(q)
                    return last
                pe.wait_ge(s["kd_ld"], 32 * (step + 1))
                pe.wait_ge(s["qm_ready"], step + 1)
                for n in range(total):
                    if split and n == total - 2:
                        run(units)
                        yield
                        if i > 3:
                            pe.wait_ge(s["ast3_ready"], i - 3)
                    pe.wait_ge(s["exp_done"], chunk(i, b, n) + 1)
                    if n == 2:
                        pe.wait_ge(s["ke_ld"], 32 * (4 * (i - 1) + b + 1))
                    if n == 2 + 2 * half:
                        pe.wait_ge(s["ke2_ld"], 32 * (4 * (i - 2) + b + 1))
                    for k, g2, hh, j in blocks(i, n):
                        keys_of = kd[64 * hh:64 * hh + KR + 2, g2, :] if n < 2 else ke[64 * hh:64 * hh + KR + 2, g2, j * P:(j + 1) * P]
                        last = mm(pb[1 + n % 2][:, k * P:(k + 1) * P], keys_of, qm[64 * hh:64 * hh + KR + 2, g2, :], start=True, stop=True)
                    last.then_inc(s["e_lg"], 1)
                    spread(2 * n)
                    if n >= 3:
                        multiply(n - 1).then_inc(s["av_done"], 1)
                    spread(2 * n + 1)
                run(units)
                if total > 2:
                    multiply(total - 1).then_inc(s["av_done"], 1)
                if after:
                    turn_maxima(*after)
                multiply(0)
                multiply(1).then_inc(s["r_done"], 1)
                pe.wait_ge(s["rT_sb"], step + 1)
                if i:
                    pe.wait_ge(s["r_evac"], step)
                for g4 in range(4):
                    last = mm(pb[3][:, 512 + g4 * P:512 + (g4 + 1) * P], rts[:, g4, :], ident, start=True, stop=True)
                last.then_inc(s["rn_ps"], 1)
            run(max_units(0, 0))
            turn_maxima(0, 0)
            def nothing(k):
                pass

            def attention_out(i, u, between):
                pe.wait_ge(s["ac_ready"], i + 1)
                for t in range(B):
                    last = mm(pb[0][:, t * P:(t + 1) * P], ac[:, t, :], ident, start=True, stop=True)
                last.then_inc(s["at_ps"], 1)
                between(0)
                pe.wait_ge(s["at_sb"], i + 1)
                for t in range(B):
                    mm(pb[0][:, 512 + t * P:512 + (t + 1) * P], aT[:, t, :], wT[:, 3, :], start=True, stop=False)
                    last = mm(pb[0][:, 512 + t * P:512 + (t + 1) * P], ones1[0:1, :], bdrow[0:1, :], start=False, stop=True)
                last.then_inc(s["y_ps"], 1)
                between(1)
                pe.wait_ge(s["h2_ready"], i + 1)
                for t in range(B):
                    last = mm(pb[0][:, t * P:(t + 1) * P], h2[:, u, t, :], ident, start=True, stop=True)
                last.then_inc(s["h2T_ps"], 1)
                between(2)

            def gates_queries(i, u, between):
                pe.wait_ge(s["h2T_sb"], i + 1)
                hx = h2T[:, :, :].rearrange("p b n -> p (b n)")
                for c in range(4):
                    if c >= 2:
                        pe.wait_ge(s["act"], 4 * i + c - 1)
                    mm(pb[1 + c % 2][:, 0:512], wT[:, 8 + c, :], hx, start=True, stop=True)
                    mm(pb[1 + c % 2][:, 512:1024], wT[:, 12 + c, :], hx, start=True, stop=True).then_inc(s["gu_ps"], 1)
                    if c:
                        between(c - 1)
                for c in range(4):
                    if c >= 2:
                        pe.wait_ge(s["q_sb"], 4 * i + c - 1)
                    mm(pb[0][:, (c % 2) * 512:(c % 2) * 512 + 512], wT[:, 4 + c, :], hx, start=True, stop=True).then_inc(s["q_ps"], 1)

            def selection(i, u, between):
                pe.wait_ge(s["act"], 4 * i + 4)
                pe.wait_ge(s["q_sb"], 4 * i + 4)
                for t in range(B):
                    if t >= 2:
                        pe.wait_ge(s["sim_red"], 4 * i + t - 1)
                    for q in range(2):
                        for h in range(RH):
                            c, e = 2 * q + h // 2, h % 2
                            last = mm(pb[1 + t % 2][:, e * 512 + c * P:e * 512 + (c + 1) * P], qT[64 * e:64 * e + 64, c, t, :],
                                      wT[64 * e:64 * e + 64, 20 + c, :], start=True, stop=True)
                    last.then_inc(s["sim_ps"], 1)
                    if t:
                        between(t - 1)
                for t in range(B):
                    for c in range(4):
                        last = mm(pb[0][:, t * P:(t + 1) * P], hid[:, c, t, :], wT[:, 16 + c, :], start=c == 0, stop=c == 3)
                last.then_inc(s["mlp_ps"], 1)

            first = None
            for i in range(NI):
                if i:
                    run(first)
                with pe.Fori(1 if i else 0, B - 1) as b:
                    run(attend(i, b, (i, b + 1)))
                run(attend(i, B - 1, (i + 1, 0) if i < NI - 1 else None))
                pe.wait_ge(s["rd_ready"], i + 1)
                mm(pb[1][0:B * H, 0:P], rdn[:, :, :].rearrange("p b h -> p (b h)"), ident, start=True, stop=True).then_inc(s["rdT_ps"], 1)
                pe.wait_ge(s["rdT_sb"], i + 1)
                if i < NI - 1:
                    first = attend(i + 1, 0, (i + 1, 1), True)
                    next(first)
                    pe.wait_ge(s["exp_done"], chunk(i + 1, 0, 2 * (i + 1) - 1) + 3)
                else:
                    attention_out(0, 0, nothing)
                    gates_queries(0, 0, nothing)
                    selection(0, 0, nothing)
                    pe.wait_ge(s["sim_red"], 4)
                pe.wait_ge(s["vt_ld"], 16 * (B + B * NC) * (i + 1))
                for c in range(NC):
                    rows = slice(c * NB, (c + 1) * NB)
                    for m in range(B):
                        wait_alone(pe, "rr_ready", 16 * i + 4 * c + m + 1, "passed_pe")
                        for h in range(H):
                            last = mm(px[m][rows, h, :], vtb[rows, m, h, :], rr[rows, m, h, :], start=True, stop=True, skip_group_check=True)
                        last.then_inc(s["px_done"], 1)
                    if c < NC - 1:
                        for m in range(B):
                            wait_alone(pe, "acur", 16 * i + 4 * c + m + 1, "passed_pe")
                            for h in range(H):
                                for to in range(c + 1, NC):
                                    last = mm(pacc[m][to * NB:(to + 1) * NB, h, :], edb[rows, m, h, to * NB:(to + 1) * NB],
                                              acur[rows, m, h, :], start=(c == 0 and h == 0), stop=True, skip_group_check=True)
                            last.then_inc(s["acc_done"], 1)
                pe.wait_ge(s["acur"], 16 * (i + 1))
            pe.sem_inc(s["pu_used"], 2)

            def unit(i, u, more):
                for t in range(B):
                    def add_up(k):
                        pe.wait_ge(s["pu_ready"], 3 * (4 * i + t) + k + 1)
                        if k == 2:
                            pe.sem_inc(s["g_free"], 1)
                        for m in range(PIECE):
                            last = mm(pb[3][:, (t % 2) * 512:(t % 2) * 512 + D], ident, pu[:, (3 * t + k) % 2, m, :],
                                      start=k == 0 and m == 0, stop=k == 2 and m == PIECE - 1)
                        last.then_inc(s["pu_used"], 1)
                    if more and t == 0:
                        attention_out(i + 1, 1 - u, add_up)
                        gates_queries(i + 1, 1 - u, nothing)
                    elif more and t == 1:
                        selection(i + 1, 1 - u, add_up)
                    else:
                        for k in range(3):
                            add_up(k)
            run_units(pe, unit)

        @block.vector
        def _(v):
            V = nc.vector
            n = [0]

            def lk(ins):
                link(v, ins, s["dve"], n)

            def restart():
                v.sem_clear(s["dve"])
                n[0] = 0
            v.wait_ge(s["w_in"], 16 * NSETUP_IN[0])
            v.wait_ge(s["c_ready"], 7)
            V.tensor_copy(identb[:, :], ident)
            lk(V.tensor_copy(maskb[:, :], cst[:, C_MASK:C_MASK + P]))
            v.wait_ge(s["wt_sb"], 1)
            for qk in range(2):
                src = wT[:, qk, :].rearrange("p (g e d) -> p e d g", g=G2, e=2)
                bsrc = wrow[0:1, qk * D:(qk + 1) * D].rearrange("p (g e d) -> p e d g", g=G2, e=2)
                for w in range(2):
                    dst = wp[:, 2 * qk + w, :].rearrange("p (e d g) -> p e d g", e=2, g=G2)
                    bdst = brow[0:1, 2 * qk + w, :].rearrange("p (e d g) -> p e d g", e=2, g=G2)
                    for dd, ss in ((dst, src), (bdst, bsrc)):
                        for e in range(2):
                            if w == 0:
                                lk(V.tensor_copy(dd[:, e], ss[:, e]))
                            else:
                                lk(V.tensor_copy(dd[:, e, 2:8], ss[:, e, 2:8]))
                                lk(V.tensor_copy(dd[:, e, 0], ss[:, e, 1]))
                                lk(V.tensor_copy(dd[:, e, 1], ss[:, e, 0]))
            v.sem_inc(s["setup_dve"], 1)
            v.wait_ge(s["silu_c"], 1)
            V.tensor_copy(scb[:, :, :], sc[:, :].unsqueeze(2).broadcast_to([P, B, P])).then_inc(s["scb"], 1)
            v.wait_ge(s["mod_sb"], B)
            for m in (1, 4):
                lk(V.tensor_scalar(mod[:, :, m, :], mod[:, :, m, :], 1.0, None, ALU.add))
            for m in (2, 5):
                lk(V.tensor_scalar(tmpm[:, :, :], mod[:, :, m, :], -1.0, 0.25, ALU.mult, ALU.max))
                lk(V.tensor_tensor(tmpm[:, :, :], tmpm[:, :, :], mod[:, :, m, :], ALU.max))
                lk(V.tensor_scalar(mod[:, :, m, :], mod[:, :, m, :], 0.0, 2.0, ALU.is_ge, ALU.mult))
                lk(V.tensor_scalar(mod[:, :, m, :], mod[:, :, m, :], -1.0, None, ALU.add))
                lk(V.tensor_tensor(mod[:, :, m, :], mod[:, :, m, :], tmpm[:, :, :], ALU.mult))
            v.wait_ge(s["bias_ps"], 1)
            lk(V.tensor_copy(bcol[:, :], pb[3][:, 0:4]))
            def normalise(b, later=True):
                for t in range(NI):
                    V.bn_stats(st[:, t, :], xs[:, b, t, :]).then_inc(s["dve"], 1)
                n[0] += NI
                v.wait_ge(s["dve"], n[0])
                for t in range(NI):
                    V.bn_aggr(mv[:, t, :], st[:, t, :]).then_inc(s["dve"], 1)
                n[0] += NI
                v.wait_ge(s["dve"], n[0])
                V.tensor_scalar(rs[:, :], mv[:, :, 1], EPS, None, ALU.add).then_inc(s["var_ready"], 1)
                v.wait_ge(s["sd_ready"], b + 1)
                lk(V.reciprocal(rs[:, :], sd[:, :]))
                if later:
                    v.wait_ge(s["hT_ps"], b)
                for t in range(NI):
                    V.tensor_scalar(hn[:, t, :], xs[:, b, t, :], mv[:, t, 0:1], rs[:, t:t + 1], ALU.subtract, ALU.mult).then_inc(s["dve"], 1)
                n[0] += NI
                v.wait_ge(s["dve"], n[0])
                lk(V.tensor_tensor(hn[:, :, :], hn[:, :, :], mod[:, b, 1:2, :].broadcast_to([P, NI, D]), ALU.mult))
                V.tensor_tensor(hn[:, :, :], hn[:, :, :], mod[:, b, 0:1, :].broadcast_to([P, NI, D]), ALU.add).then_inc(s["h_ready"], 1)

            def rotate_split(b, more):
                restart()
                if more:
                    normalise(b + 1)
                for qk, res in ((0, qf), (1, kf)):
                    v.wait_ge(s["proj"], 2 * b + qk + 1)
                    V.scalar_tensor_tensor(t1[:, :], pb[1][:, :], bcol[:, 2 * qk:2 * qk + 1], cst[:, C_COS:C_COS + S], ALU.add, ALU.mult).then_inc(s["dve"], 1)
                    V.scalar_tensor_tensor(t2[:, :], pb[2][:, :], bcol[:, 2 * qk + 1:2 * qk + 2], cst[:, C_SIN:C_SIN + S], ALU.add, ALU.mult).then_inc(s["dve"], 1)
                    n[0] += 2
                    v.wait_ge(s["dve"], n[0])
                    lk(V.tensor_tensor(res[:, :], t1[:, :], t2[:, :], ALU.add))
                    v.sem_inc(s["rope"], 1)
                    if qk == 0:
                        v.wait_ge(s["parts_st"], 16 * 24 * b + 16)
                    lk(V.tensor_copy(qkp[:, qk, 0, :], res[:, :]))
                    lk(V.tensor_tensor(t1[:, :], res[:, :], qkp[:, qk, 0, :], ALU.subtract))
                    lk(V.tensor_copy(qkp[:, qk, 1, :], t1[:, :]))
                    V.tensor_tensor(qkp[:, qk, 2, :], t1[:, :], qkp[:, qk, 1, :], ALU.subtract).then_inc(s["parts"], 1)
                    v.wait_ge(s["parts"], 2 * b + qk + 1)
                V.tensor_tensor(prod[:, :], qf[:, :], kf[:, :], ALU.mult).then_inc(s["prod_ready"], 1)
                v.wait_ge(s["prod_ready"], b + 1)
            restart()
            normalise(0, False)
            with v.Fori(0, B - 1) as b:
                rotate_split(b, True)
            rotate_split(B - 1, False)
            v.wait_ge(s["parts_st"], 16 * 24 * B + 16)
            v.sem_inc(s["a_ready"], 1)
            mrow = mx[:, :, :].rearrange("p g (e c) -> p g e c", e=2)
            restart()
            v.wait_ge(s["ld_sb"], B)
            lk(V.memset(pb[3][:, 0:512], 0.0))

            def maxima(i, b):
                nch = 1 if i < 4 else 2
                for k, (heads, c0) in enumerate(max_parts(i)):
                    w = min(512, (i + 1) * P - c0)
                    v.wait_ge(s["max_lg"], mlg(i, b, k) + 1)
                    V.reduce_max(mraw[:, heads[0]:heads[-1] + 1:2, c0 // 512], pb[0][:, (k % 2) * 512:(k % 2) * 512 + len(heads) * w].rearrange("p (h n) -> p h n", n=w),
                                 AX.X).then_inc(s["max_red"], 1)
                v.wait_ge(s["max_red"], mlg(i, b, mcount(i)))
                if nch == 2:
                    lk(V.tensor_tensor(mfin[:, :], mraw[:, :, 0], mraw[:, :, 1], ALU.max))
                else:
                    lk(V.tensor_copy(mfin[:, :], mraw[:, :, 0]))
                mf = mfin[:, :].rearrange("p (g e) -> p g e", e=2)
                lk(V.tensor_scalar(mrow[:, :, :, KR], mf, -1.0, None, ALU.mult))
                lk(V.scalar_tensor_tensor(mrow[:, :, :, KR + 1], mf, -1.0, mrow[:, :, :, KR], ALU.mult, ALU.subtract))
                eb = esub[:, b, :].rearrange("p (g e) -> p g e", e=2)
                lb = ldg[:, b, i, :].rearrange("p (g e) -> p g e", e=2)
                if i:
                    v.wait_ge(s["es_ready"], i)
                lk(V.tensor_tensor(eb, lb, mrow[:, :, :, KR], ALU.add))
                V.tensor_tensor(eb, eb, mrow[:, :, :, KR + 1], ALU.add).then_inc(s["mx_ready"], 1)

            def shifted_queries(i, b):
                v.wait_ge(s["mT_done"], 4 * i + b + 1)
                V.tensor_tensor(qm[:, :, :].rearrange("p g n -> p (g n)"), qa[:, :, :].rearrange("p g n -> p (g n)"), pb[0][:, :], ALU.add).then_inc(s["qm_ready"], 1)

            def turn_back(i, b):
                v.wait_ge(s["rn_ps"], 4 * i + b + 1)
                V.tensor_copy(rsb[:, b, :, :].rearrange("p (g q) d -> p g q d", g=4), rback[:, :, :, 0:HD + 1]).then_inc(s["r_evac"], 1)

            def attend_dve(i, b, after):
                restart()
                if after:
                    maxima(*after)
                    shifted_queries(*after)
                turn_back(i, b)
            def attention_out(i, u):
                v.wait_ge(s["y_ps"], i + 1)
                lk(V.tensor_tensor(tf, pb[0][:, 512:1024].rearrange("p (b d) -> p b d", b=B), mod[:, :, 2, :], ALU.mult))
                lk(V.tensor_tensor(xs[:, :, i, :], xs[:, :, i, :], tf, ALU.add))
                for t in range(B):
                    V.bn_stats(st2[:, t, :], xs[:, t, i, :]).then_inc(s["dve"], 1)
                n[0] += B
                v.wait_ge(s["dve"], n[0])
                for t in range(B):
                    V.bn_aggr(mv2[:, t, :], st2[:, t, :]).then_inc(s["dve"], 1)
                n[0] += B
                v.wait_ge(s["dve"], n[0])
                V.tensor_scalar(rs2[:, :], mv2[:, :, 1], EPS, None, ALU.add).then_inc(s["var2"], 1)
                v.wait_ge(s["sd2"], i + 1)
                lk(V.reciprocal(rs2[:, :], sd2[:, :]))
                for t in range(B):
                    V.tensor_scalar(h2[:, u, t, :], xs[:, t, i, :], mv2[:, t, 0:1], rs2[:, t:t + 1], ALU.subtract, ALU.mult).then_inc(s["dve"], 1)
                n[0] += B
                v.wait_ge(s["dve"], n[0])
                lk(V.tensor_tensor(h2[:, u, :, :], h2[:, u, :, :], mod[:, :, 4, :], ALU.mult))
                V.tensor_tensor(h2[:, u, :, :], h2[:, u, :, :], mod[:, :, 3, :], ALU.add).then_inc(s["h2_ready"], 1)

            def gates(i, u):
                for c in range(4):
                    v.wait_ge(s["sg"], 4 * i + c + 1)
                    V.tensor_tensor(hid[:, c, :, :].rearrange("p b n -> p (b n)"), sg[:, c % 2, :], pb[1 + c % 2][:, 512:1024], ALU.mult).then_inc(s["act"], 1)

            def best_keys(i, u):
                for t in range(B):
                    wait_alone(v, "sim_ps", 4 * i + t + 1, "passed_dve")
                    for q in range(2):
                        for h in range(RH):
                            c, e = 2 * q + h // 2, h % 2
                            V.max(sv[:, q, t, h, :], pb[1 + t % 2][:, e * 512 + c * P:e * 512 + (c + 1) * P]).then_inc(s["dve"], 1)
                    n[0] += 8
                    v.wait_ge(s["dve"], n[0])
                    for q in range(2):
                        for h in range(RH):
                            c, e = 2 * q + h // 2, h % 2
                            last = V.max_index(iv[:, q, t, h, :], sv[:, q, t, h, :], pb[1 + t % 2][:, e * 512 + c * P:e * 512 + (c + 1) * P])
                    last.then_inc(s["sim_red"], 1)
                v.wait_ge(s["sim_red"], 4 * i + 4)

            def selection(i, u):
                TH = B * RH
                svx = sv[:, 0].rearrange("p t h k -> p (t h) k").unsqueeze(3).broadcast_to([P, TH, TOPK, TOPK])
                svy = sv[:, 1].rearrange("p t h k -> p (t h) k").unsqueeze(2).broadcast_to([P, TH, TOPK, TOPK])
                lk(V.tensor_tensor(allsc, svx, svy, ALU.add))
                lk(V.tensor_copy(ivf[:, :, :, :].rearrange("p q t k -> p (q t k)"), iv[:, :, :, :, :].rearrange("p q t h k -> p (q t h k)")))
                for m in range(TH):
                    V.max(scs[:, m, :], allsc[:, m].rearrange("p a c -> p (a c)")).then_inc(s["dve"], 1)
                n[0] += TH
                v.wait_ge(s["dve"], n[0])
                for m in range(TH):
                    V.max_index(pos[:, m, :], scs[:, m, :], allsc[:, m].rearrange("p a c -> p (a c)")).then_inc(s["dve"], 1)
                n[0] += TH
                v.wait_ge(s["dve"], n[0])
                V.tensor_tensor(wsub[:, :, :], scs[:, :, :], scs[:, :, 0:1].broadcast_to([P, TH, TOPK]), ALU.subtract).then_inc(s["sub_ready"], 1)
                yield
                pf = pos[:, :, :].rearrange("p m k -> p (m k)")
                lk(V.tensor_scalar(pab[:, 0, :], pf, 3, None, ALU.logical_shift_right))
                lk(V.tensor_scalar(pab[:, 1, :], pf, 7, None, ALU.bitwise_and))
                lk(V.tensor_copy(pabf[:, :, :], pab[:, :, :]))
                for q in range(2):
                    lk(V.tensor_tensor(oh, pabf[:, q, :].unsqueeze(2).broadcast_to([P, TH * TOPK, TOPK]),
                                       cst[:, C_IOTA:C_IOTA + TOPK].unsqueeze(1).broadcast_to([P, TH * TOPK, TOPK]), ALU.is_equal))
                    o4 = oh.rearrange("p (m k) a -> p m k a", k=TOPK)
                    lk(V.tensor_tensor(o4, o4, ivf[:, q].unsqueeze(2).broadcast_to([P, TH, TOPK, TOPK]), ALU.mult))
                    lk(V.reduce_sum(isel[:, q, :], oh, AX.X))
                    yield
                lk(V.scalar_tensor_tensor(ef[:, :], isel[:, 0, :], float(NKEY), isel[:, 1, :], ALU.mult, ALU.add))
                lk(V.tensor_scalar(ef[:, :], ef[:, :], float(NEXP - 1), None, ALU.min))
                V.tensor_copy(ei[:, u, :], ef[:, :]).then_inc(s["idx_ready"], 1)
                v.wait_ge(s["mlp_ps"], i + 1)
                lk(V.tensor_tensor(tf, pb[0][:, 0:512].rearrange("p (b d) -> p b d", b=B), mod[:, :, 5, :], ALU.mult))
                lk(V.tensor_tensor(xs[:, :, i, :], xs[:, :, i, :], tf, ALU.add))
                v.wait_ge(s["ex_ready"], i + 1)
                lk(V.reduce_sum(wsum[:, :], wex[:, :, :], AX.X))
                lk(V.reciprocal(wrs[:, :], wsum[:, :]))
                lk(V.tensor_tensor(wex[:, :, :], wex[:, :, :], wrs[:, :].unsqueeze(2).broadcast_to([P, TH, TOPK]), ALU.mult))
                wf = wex[:, :, :].rearrange("p (t h) k -> p t (h k)", t=B)
                lk(V.scalar_tensor_tensor(coef[:, u, :, 0:SLOTS - 1], ef[:, :].rearrange("p (t m) -> p t m", t=B), NEXP - 1.5, wf, ALU.is_lt, ALU.mult))
                lk(V.tensor_tensor(wf, wf, coef[:, u, :, 0:SLOTS - 1], ALU.subtract))
                lk(V.reduce_sum(coef[:, u, :, SLOTS - 1:SLOTS], wf, AX.X))

            maxima(0, 0)
            shifted_queries(0, 0)
            for i in range(NI):
                if i:
                    shifted_queries(i, 1)
                    turn_back(i, 0)
                with v.Fori(1 if i else 0, B - 1) as b:
                    attend_dve(i, b, (i, b + 1))
                attend_dve(i, B - 1, (i + 1, 0) if i < NI - 1 else None)
                restart()
                v.wait_ge(s["r_evac"], 4 * (i + 1))
                V.reciprocal(rdn[:, :, :], rsb[:, :, :, HD]).then_inc(s["rd_ready"], 1)
                v.wait_ge(s["es_ready"], i + 1)
                v.wait_ge(s["rd_ready"], i + 1)
                v.wait_ge(s["rdT_ps"], i + 1)
                V.tensor_copy(rdT[:, :], pb[1][0:B * H, 0:P]).then_inc(s["rdT_sb"], 1)
                lk(V.tensor_tensor(rn[:, :, :, :], v_all[:, :, i, :, :], es[:, :, :].unsqueeze(3).broadcast_to([P, B, H, HD]), ALU.mult))
                lk(V.tensor_tensor(rn[:, :, :, :], rn[:, :, :, :], rsb[:, :, :, 0:HD], ALU.add))
                lk(V.tensor_tensor(rn[:, :, :, :], rn[:, :, :, :], rdn[:, :, :].unsqueeze(3).broadcast_to([P, B, H, HD]), ALU.mult))
                if i:
                    v.wait_ge(s["z_st"], 16 * i)
                lk(V.memset(zb[:, :, :, :], 0.0))
                for e in range(2):
                    lk(V.memset(zb[:, e, :, :].rearrange("p k i -> p (k i)")[:, 0:NB * NB:NB + 1], 1.0))
                if i == NI - 1:
                    attention_out(0, 0)
                v.wait_ge(s["x_ld"], 16 * 16 * (i + 1))
                v.wait_ge(s["r_ld"], 16 * (i + 1))
                lk(V.tensor_tensor(xb[:, :, :, :], xb[:, :, :, :], rdb[:, :, :].unsqueeze(2).broadcast_to([P, 2, NB, NB]), ALU.mult))
                for j in range(NB - 1):
                    w, u = NB - 1 - j, j + 1
                    for e in range(2):
                        if j:
                            v.wait_ge(s["dve"], n[0] - 1)
                        V.tensor_tensor(tb[:, e, 0:u, 0:w], xb[:, e, j:j + 1, u:].broadcast_to([P, u, w]),
                                        zb[:, e, 0:u, j:j + 1].broadcast_to([P, u, w]), ALU.mult).then_inc(s["dve"], 1)
                        n[0] += 1
                    for e in range(2):
                        v.wait_ge(s["dve"], n[0] - 1)
                        V.tensor_tensor(zb[:, e, 0:u, u:], zb[:, e, 0:u, u:], tb[:, e, 0:u, 0:w], ALU.add).then_inc(s["dve"], 1)
                        n[0] += 1
                v.wait_ge(s["dve"], n[0])
                v.sem_inc(s["z_ready"], 1)
                restart()
                if i < NI - 1:
                    maxima(i + 1, 1)
                else:
                    gates(0, 0)
                    best_keys(0, 0)
                    left = selection(0, 0)
                for c in range(NC):
                    rows = slice(c * NB, (c + 1) * NB)
                    for b in range(B):
                        if c == 0:
                            V.tensor_copy(rr[rows, b, :, :], rn[rows, b, :, :]).then_inc(s["rr_ready"], 1)
                        else:
                            v.wait_ge(s["acc_done"], 12 * i + 4 * (c - 1) + b + 1)
                            lk(V.tensor_tensor(rr[rows, b, :, :], pacc[b][rows, :, :], rdn[rows, b, :].unsqueeze(2).broadcast_to([NB, H, HD]), ALU.mult))
                            V.tensor_tensor(rr[rows, b, :, :], rr[rows, b, :, :], rn[rows, b, :, :], ALU.add).then_inc(s["rr_ready"], 1)
                    if i == NI - 1 and c < NC - 1:
                        next(left)
                if i == NI - 1:
                    run(left)
                for b in range(B):
                    v.wait_ge(s["acur"], 16 * i + 13 + b)
                    V.tensor_copy(a_all[:, b, i, :, 0:HD], acur[:, b, :, :]).then_inc(s["a_ready"], 1)

            def finish(i, t):
                v.wait_ge(s["pu_used"], 3 * (4 * i + t) + 5)
                v.wait_ge(s[out_st[t % 2]], 16 * (2 * i + t // 2 + 1))
                lk(V.tensor_tensor(ot[:, t % 2, :], pb[3][:, (t % 2) * 512:(t % 2) * 512 + D], mod[:, t, 5, :], ALU.mult))
                V.tensor_tensor(ot[:, t % 2, :], ot[:, t % 2, :], xs[:, t, i, :], ALU.add).then_inc(s["out_ready"], 1)

            def unit(i, u, more):
                if u == 0:
                    restart()
                for t in range(B):
                    v.wait_ge(s[gathered[t % 2]], 16 * (SLOTS - 1) * (2 * i + t // 2 + 1))
                    for k in range(3):
                        part = slice(k * PIECE, (k + 1) * PIECE)
                        lk(V.tensor_tensor(pr[:, :, :], gbuf[:, t % 2, part, 0:D], h2[:, u, t:t + 1, :].broadcast_to([P, PIECE, D]), ALU.mult))
                        ins = V.reduce_sum(wd_s[:, part], pr[:, :, :], AX.X)
                        if k < 2:
                            lk(ins)
                        else:
                            ins.then_inc(s["dots"], 1)
                    v.wait_ge(s["silu_w"], 4 * i + t + 1)
                    V.tensor_tensor(wc[:, t % 2, :], ws[:, :], coef[:, u, t, :], ALU.mult).then_inc(s["wc_ready"], 1)
                    if t:
                        finish(i, t - 1)
                    if more and t == 0:
                        attention_out(i + 1, 1 - u)
                        gates(i + 1, 1 - u)
                    if more and t == 1:
                        best_keys(i + 1, 1 - u)
                    if more and t == 2:
                        run(selection(i + 1, 1 - u))
                finish(i, B - 1)
            V.memset(gbuf[:, 1, :, :], 0.0).then_inc(s["g_clear"], 1)
            run_units(v, unit)


def kernel(**inputs):
    import numpy as np
    import concourse.bacc as _bacc
    from concourse.bass_utils import run_bass_kernel_spmd as _run

    nc = _bacc.Bacc("TRN2", target_bir_lowering=False, num_devices=1)
    names = ["L0_attn_hidden_states", "L0_attn_Wqkv", "L0_attn_bqkv", "L0_attn_Wd", "L0_attn_bd", "L0_ffn_Wq", "L0_ffn_keys",
             "L0_ffn_down_embed", "L0_ffn_up_embed", "L0_ffn_Wg", "L0_ffn_Wu", "L0_ffn_Wd", "L0_c", "L0_wmod"]
    arrays = {n: np.ascontiguousarray(inputs[n]) for n in names}
    arrays["constants"] = constants()
    args = [nc.dram_tensor(n, a.shape, mybir.dt.from_np(a.dtype), kind="ExternalInput").ap() for n, a in arrays.items()]
    args.append(nc.dram_tensor("out", (B, S, D), F32, kind="ExternalOutput").ap())
    adaln_block(nc, *args)
    r = _run(nc, [arrays], core_ids=[0])
    return r.results[0]["out"]
```
